# Optimizing a Trainium2 kernel written in Bass

```python
import numpy as np
import jax
import jax.numpy as jnp

def _softmax(x, axis=-1):
    return jax.nn.softmax(x, axis=axis)

def _gelu(x):
    return jax.nn.gelu(x, approximate=True)

def _silu(x):
    return jax.nn.silu(x)

def _sigmoid(x):
    return jax.nn.sigmoid(x)

def _layernorm(x, axis=-1, eps=1e-05):
    m = jnp.mean(x, axis=axis, keepdims=True)
    v = jnp.var(x, axis=axis, keepdims=True)
    return (x - m) / jnp.sqrt(v + eps)

def _scatter_add(tgt, idx, src, axis=0):
    return tgt.at[idx].add(src)

def _segment_sum(src, seg, n):
    return jax.ops.segment_sum(src, seg, n)
kernel_name = 'mk_vit_tower_d1_tok_img4096_r4_4be77d'

def setup_inputs(seed: int=0):
    np.random.seed(seed)
    _w = jnp.asarray

    def _rec_inputs():
        import jax
        import jax.numpy as jnp
        _rk = jax.random.key(seed)
        x = -0.0043416 + 0.998921 * jax.random.normal(jax.random.fold_in(_rk, 1), (64, 64, 64, 2), jnp.float32)
        return x
    x = _rec_inputs()

    def _L0_tok_setup():
        import jax, jax.numpy as jnp
        import numpy as np
        H, N, CH = (64, 64, 1)
        key = jax.random.key(seed)
        k1, k2, k3 = jax.random.split(key, 3)
        A_abslog = jnp.log(jax.random.uniform(k1, (H, N), dtype=jnp.float32, minval=0.5, maxval=0.999))
        A_phase = jax.random.uniform(k2, (H, N), dtype=jnp.float32, minval=-np.pi, maxval=np.pi)
        C = jax.random.normal(k3, (CH, H, N, 2), dtype=jnp.float32)
        return {'A_abslog': A_abslog, 'A_phase': A_phase, 'C': C, 'L': 1024}
    _L0_tok_all = _L0_tok_setup()
    _L0_tok_in = {k: v for k, v in _L0_tok_all.items() if k in ('A_abslog', 'A_phase')}
    del _L0_tok_all

    def _L0_attn_setup():
        import math
        import jax, jax.numpy as jnp
        import numpy as np
        NUM_HEADS = 32
        HIDDEN = 1024
        HEAD_DIM = HIDDEN // NUM_HEADS
        NEG_INF = -1e+30

        def _alibi_slopes(n: int) -> jnp.ndarray:
            cp2 = 2 ** math.floor(math.log2(n))
            base = 2.0 ** (-2.0 ** (-(math.log2(cp2) - 3)))
            slopes = base ** np.arange(1, cp2 + 1, dtype=np.float64)
            if cp2 != n:
                extra_base = 2.0 ** (-2.0 ** (-(math.log2(2 * cp2) - 3)))
                rem = min(cp2, n - cp2)
                extra = extra_base ** np.arange(1, 1 + 2 * rem, 2, dtype=np.float64)
                slopes = np.concatenate([slopes, extra])
            return jnp.asarray(slopes, dtype=jnp.float32)
        key = jax.random.key(seed)
        k1, k2, k3 = jax.random.split(key, 3)
        B, S = (2, 512)
        hidden_states = jax.random.normal(k1, (B, S, HIDDEN), dtype=jnp.float32)
        Wqkv = jax.random.normal(k2, (HIDDEN, NUM_HEADS * HEAD_DIM + 2 * HEAD_DIM), dtype=jnp.float32) * 0.02
        Wo = jax.random.normal(k3, (HIDDEN, HIDDEN), dtype=jnp.float32) * 0.02
        return {'hidden_states': hidden_states, 'Wqkv': Wqkv, 'Wo': Wo}
    _L0_attn_all = _L0_attn_setup()
    _L0_attn_in = {k: v for k, v in _L0_attn_all.items() if k in ('Wqkv', 'Wo')}
    del _L0_attn_all

    def _L0_ffn_setup():
        import jax, jax.numpy as jnp
        import numpy as np
        IN_F = 1024
        OUT_F = 1024
        RANK = 8
        NUM_EXPERTS = 64
        TOP_K = 16
        ROUTER_DIM = 16
        ALPHA = 32
        SCALING = ALPHA / TOP_K
        BOTTLENECK = NUM_EXPERTS * RANK
        key = jax.random.key(seed)
        ks = jax.random.split(key, 5)
        x = jax.random.normal(ks[0], (4, 1024, IN_F), dtype=jnp.float32)
        bound_a = float(np.sqrt(6.0 / IN_F))
        A_w = jax.random.uniform(ks[1], (BOTTLENECK, IN_F), jnp.float32, -bound_a, bound_a)
        B_w = jax.random.normal(ks[2], (OUT_F, BOTTLENECK), dtype=jnp.float32) * 0.02
        Wq_w = jax.random.normal(ks[3], (ROUTER_DIM, IN_F), dtype=jnp.float32) * 0.02
        keys = jax.random.normal(ks[4], (NUM_EXPERTS, ROUTER_DIM), dtype=jnp.float32) * 0.01
        return {'x': x, 'A_w': A_w, 'B_w': B_w, 'Wq_w': Wq_w, 'keys': keys}
    _L0_ffn_all = _L0_ffn_setup()
    _L0_ffn_in = {k: v for k, v in _L0_ffn_all.items() if k in ('A_w', 'B_w', 'Wq_w', 'keys')}
    del _L0_ffn_all
    return {'x': x, 'L0_tok_A_abslog': _L0_tok_in['A_abslog'], 'L0_tok_A_phase': _L0_tok_in['A_phase'], 'L0_attn_Wqkv': _L0_attn_in['Wqkv'], 'L0_attn_Wo': _L0_attn_in['Wo'], 'L0_ffn_A_w': _L0_ffn_in['A_w'], 'L0_ffn_B_w': _L0_ffn_in['B_w'], 'L0_ffn_Wq_w': _L0_ffn_in['Wq_w'], 'L0_ffn_keys': _L0_ffn_in['keys']}

def reference(x, L0_tok_A_abslog, L0_tok_A_phase, L0_attn_Wqkv, L0_attn_Wo, L0_ffn_A_w, L0_ffn_B_w, L0_ffn_Wq_w, L0_ffn_keys):
    import jax
    import jax.numpy as jnp

    def _L0_tok_ref(A_abslog, A_phase, C, L):
        import jax, jax.numpy as jnp
        import numpy as np
        H, N, CH = (64, 64, 1)
        A = jnp.exp(A_abslog + 1j * A_phase)
        dtA = jnp.log(A)
        Cc = C[..., 0] + 1j * C[..., 1]
        Cc = Cc * (A - 1.0) / dtA
        t = jnp.arange(L, dtype=jnp.float32)
        K = jnp.exp(dtA[:, :, None] * t)
        K = jnp.einsum('chn,hnl->chl', Cc, K)
        return 2.0 * K.real

    def _L0_attn_ref(hidden_states, Wqkv, Wo):
        import math
        import jax, jax.numpy as jnp
        import numpy as np
        NUM_HEADS = 32
        HIDDEN = 1024
        HEAD_DIM = HIDDEN // NUM_HEADS
        NEG_INF = -1e+30

        def _alibi_slopes(n: int) -> jnp.ndarray:
            cp2 = 2 ** math.floor(math.log2(n))
            base = 2.0 ** (-2.0 ** (-(math.log2(cp2) - 3)))
            slopes = base ** np.arange(1, cp2 + 1, dtype=np.float64)
            if cp2 != n:
                extra_base = 2.0 ** (-2.0 ** (-(math.log2(2 * cp2) - 3)))
                rem = min(cp2, n - cp2)
                extra = extra_base ** np.arange(1, 1 + 2 * rem, 2, dtype=np.float64)
                slopes = np.concatenate([slopes, extra])
            return jnp.asarray(slopes, dtype=jnp.float32)
        B, S, H = hidden_states.shape
        nH, d = (NUM_HEADS, HEAD_DIM)
        scale = d ** (-0.5)
        qkv = hidden_states @ Wqkv
        q = qkv[..., :nH * d].reshape(B, S, nH, d)
        k = qkv[..., nH * d:nH * d + d]
        v = qkv[..., nH * d + d:]
        scores = jnp.einsum('bqhd,bkd->bhqk', q, k) * scale
        pos_q = jnp.arange(S)[:, None]
        pos_k = jnp.arange(S)[None, :]
        slopes = _alibi_slopes(nH)
        alibi = slopes[:, None, None] * (pos_k - pos_q).astype(jnp.float32)
        causal = pos_k <= pos_q
        scores = jnp.where(causal[None, None], scores + alibi[None], NEG_INF)
        probs = jax.nn.softmax(scores, axis=-1)
        attn = jnp.einsum('bhqk,bkd->bqhd', probs, v).reshape(B, S, H)
        return attn @ Wo

    def _L0_ffn_ref(x, A_w, B_w, Wq_w, keys):
        import jax, jax.numpy as jnp
        import numpy as np
        IN_F = 1024
        OUT_F = 1024
        RANK = 8
        NUM_EXPERTS = 64
        TOP_K = 16
        ROUTER_DIM = 16
        ALPHA = 32
        SCALING = ALPHA / TOP_K
        BOTTLENECK = NUM_EXPERTS * RANK
        q = jnp.einsum('bsd,rd->bsr', x, Wq_w)
        scores = jnp.einsum('bsr,er->bse', q, keys)
        top_vals, top_idx = jax.lax.top_k(scores, TOP_K)
        top_w = jax.nn.softmax(top_vals, axis=-1)
        gate = jnp.sum(jax.nn.one_hot(top_idx, NUM_EXPERTS, dtype=top_w.dtype) * top_w[..., None], axis=-2)
        z = jnp.einsum('bsd,nd->bsn', x, A_w)
        z = z.reshape(*z.shape[:-1], NUM_EXPERTS, RANK)
        z_gated = (z * gate[..., None]).reshape(*z.shape[:-2], BOTTLENECK)
        out = jnp.einsum('bsn,on->bso', z_gated, B_w) * SCALING
        return out
    h = _L0_tok_ref(L0_tok_A_abslog, L0_tok_A_phase, x, 1024)
    h = h + _L0_attn_ref(_layernorm(h, axis=-1), L0_attn_Wqkv, L0_attn_Wo)
    h = h + _L0_ffn_ref(_layernorm(h, axis=-1), L0_ffn_A_w, L0_ffn_B_w, L0_ffn_Wq_w, L0_ffn_keys)
    return h

_drawn_inputs = setup_inputs


def setup_inputs(seed=0):
    import zlib

    import numpy as np

    out = dict(_drawn_inputs(seed))
    spreads = {}
    factors = {}
    for name, (base, spread) in spreads.items():
        noise = np.random.default_rng([zlib.crc32(name.encode()), seed]).standard_normal(out[name].shape)
        drawn = base * np.exp(spread * noise) if base else spread * noise
        out[name] = jnp.asarray(drawn.astype(out[name].dtype))
    for name, factor in factors.items():
        out[name] = (out[name] * factor).astype(out[name].dtype)
    return out
```

```python
import math
from contextlib import ExitStack

import numpy as np

import concourse.bass as bass
from concourse import mybir

F32 = mybir.dt.float32
F16 = mybir.dt.float16
I32 = mybir.dt.int32
ALU = mybir.AluOpType
ACT = mybir.ActivationFunctionType
AX = mybir.AxisListType.X
RMAX = bass.bass_isa.ReduceOp.max

P = 128
BATCH, SEQ, HID = 64, 64, 1024
MODES = 64
HEADS, DH = 32, 32
NE, RANK, TOPK, RDIM = 64, 8, 16, 16
BOT = NE * RANK
KT = HID // P
ZT = BOT // P
TILES = BATCH * SEQ // P
EPS = 1e-5
SOFT_SCALE = DH ** -0.5
FFN_SCALE = 32 / TOPK
HALF = 512

NQ, NA, NB = 4, 16, 16
TK = NA + NB + NQ
HC = 4
CHUNKS = SEQ // HC
MID = 4
ROUND = 12582912.0
TWO_PI_HI = 6.28125
TWO_PI_LO = 2 * math.pi - TWO_PI_HI
PI_SAFE = 3.1415925
TAKEN = -3.0e38

FIRST, LAST = -1, TILES + 1
STEADY = (3, TILES - 2)


def has(part, i):
    lo, hi = {"next": (-1, TILES - 2), "attn": (0, TILES - 1), "proj": (1, TILES), "ffn": (2, TILES + 1)}[part]
    return lo <= i <= hi


BANKS = {
    "turn": [("x2_0", "ffn"), ("x2_1", "ffn"), ("qT_0", "attn"), ("qT_1", "attn"),
             ("zT", "ffn"), ("x1_0", "next"), ("x1_1", "next")],
    "wide0": [("q_0", "attn"), ("z", "ffn"), ("f_1", "ffn"), ("o_1", "proj")],
    "wide1": [("q_1", "attn"), ("f_0", "ffn"), ("o_0", "proj")],
    "small": [("kv", "attn"), ("kT", "attn"), ("r", "ffn")],
    "sc0": [("s_0", "attn"), ("p_0", "attn"), ("a_0", "attn")],
    "sc1": [("s_1", "attn"), ("p_1", "attn"), ("a_1", "attn")],
    "sc2": [("s_2", "attn"), ("p_2", "attn")],
    "sc3": [("s_3", "attn"), ("p_3", "attn")],
}
BANK_OF = {user: bank for bank, users in BANKS.items() for user, _ in users}


def uses_before(user, i):
    users = BANKS[BANK_OF[user]]
    at = [u for u, _ in users].index(user)
    if not isinstance(i, int):
        return (i - STEADY[0]) * len(users) + uses_before(user, STEADY[0])
    return (sum(has(part, j) for j in range(FIRST, i) for _, part in users)
            + sum(has(part, i) for _, part in users[:at]))


def wait(eng, sem, value):
    if isinstance(value, int) and value <= 0:
        return
    eng.wait_ge(sem, value)


def steps(eng, body):
    for i in range(FIRST, STEADY[0]):
        body(i, lambda part, i=i: has(part, i))
    with eng.Fori(STEADY[0], STEADY[1]) as i:
        body(i, lambda part: True)
    for i in range(STEADY[1], LAST + 1):
        body(i, lambda part, i=i: has(part, i))


def vit_layer(nc, x, abslog, phase, wqkv, wo, aw, bw, wq, keys,
              ident_c, alibi_c, times_c, turns_c, out):
    ctx = ExitStack()
    with ctx:
        def sb(name, shape, dt=F32):
            return ctx.enter_context(nc.sbuf_tensor(name, shape, dt))

        def sem(name):
            return ctx.enter_context(nc.semaphore(name))

        h_dram = nc.dram_tensor("h_rows", [BATCH * SEQ, HID], F32, kind="Internal").ap()

        QKV = HID + 2 * DH
        wqkv_s = sb("wqkv_s", [P, 2, KT, QKV], F16)
        wa_s = sb("wa_s", [P, 2, KT, BOT], F16)
        wr_s = sb("wr_s", [P, 2, KT, NE], F16)
        wb_s = sb("wb_s", [P, 2, ZT, HID], F16)
        stage = sb("stage", [P, KT * QKV])
        ident = sb("ident", [P, P])
        scales = sb("scales", [P, 5, 8])
        consts = sb("consts", [P, 8])
        keys_s = sb("keys_s", [P, RDIM])
        keysT_s = sb("keysT_s", [RDIM, NE])
        wq_s = sb("wq_s", [RDIM, HID])
        QW, OW, AW, BW, RW = range(5)

        ARENA = 25800
        arena = sb("arena", [P, ARENA])
        top = [0]

        def take(cols, dt=F32, rows=P):
            at = top[0]
            n = cols if dt == F32 else (cols + 1) // 2
            top[0] += n
            assert top[0] <= ARENA, top[0]
            v = arena[0:rows, at:at + n]
            return v if dt == F32 else v.bitcast(dt)

        al_s, ph_s = take(MODES, rows=SEQ), take(MODES, rows=SEQ)
        xin = [take(HC * 2 * MODES, rows=BATCH) for _ in range(2)]
        aT, phT = take(SEQ), take(SEQ)
        g4 = take(8 * SEQ).rearrange("p (k h) -> p k h", k=8)
        times = take(TK)
        turns = take(2 * TK).rearrange("p (v k) -> p v k", v=2)
        vtab = [take(SEQ * TK).rearrange("p (h k) -> p h k", k=TK) for _ in range(2)]
        gtab = [take(SEQ * NQ).rearrange("p (h q) -> p h q", q=NQ) for _ in range(2)]
        RW_ = NA * NB
        DW_ = NQ * BATCH
        r_part = [[take(HC * RW_) for _ in range(2)] for _ in range(2)]
        d_part = [[take(HC * DW_) for _ in range(2)] for _ in range(2)]
        r_full = [take(HC * RW_) for _ in range(2)]
        d_full = [take(HC * DW_) for _ in range(2)]
        krow = [take(HC * HALF) for _ in range(2)]
        th = stage[:, 0:SEQ * TK].rearrange("p (h k) -> p h k", k=TK)
        turn_n = stage[:, SEQ * TK:2 * SEQ * TK].rearrange("p (h k) -> p h k", k=TK)
        etab = stage[:, 2 * SEQ * TK:3 * SEQ * TK].rearrange("p (h k) -> p h k", k=TK)

        top[0] = 0
        wo_s = take(2 * KT * HID, F16).rearrange("p (s k n) -> p s k n", s=2, k=KT)
        h_in = take(HID)
        h_res = take(HID)
        h_mid = take(HID)
        h_out = take(HID)
        xn1, xn2 = h_in, take(HID)
        x1T = take(2 * HID, F16).rearrange("p (s k t) -> p s k t", s=2, k=KT)
        x2T = take(2 * HID, F16).rearrange("p (s k t) -> p s k t", s=2, k=KT)
        attT = take(2 * HID, F16).rearrange("p (s k t) -> p s k t", s=2, k=KT)
        zT = take(2 * BOT, F16).rearrange("p (s k t) -> p s k t", s=2, k=ZT)
        q_then_p = take(HEADS * SEQ)
        q_row = q_then_p[:, 0:HID]
        qT = q_then_p[:, HID:2 * HID].rearrange("p (g t) -> p g t", g=KT)
        pT = q_then_p.rearrange("p (u t) -> p u t", t=P)
        k_rep = take(4 * DH)
        k_blk = take(2 * 4 * SEQ).rearrange("p (b j k) -> p b j k", b=2, j=4)
        v_blk = take(2 * 2 * DH).rearrange("p (b m) -> p b m", b=2)
        probs = take(HEADS * SEQ)
        alibi = take(HEADS * SEQ)
        smax, ssum, srec = take(HEADS), take(HEADS), take(HEADS)
        zg = take(BOT)
        bn = take(24).rearrange("p (l k) -> p l k", l=2)
        mv = take(4).rearrange("p (l k) -> p l k", l=2)
        rs = take(16).rearrange("p (l k) -> p l k", l=2)
        half_neg = take(1)
        r_sc, r_w1, r_w2, r_sel, r_exp, r_gate = (take(NE) for _ in range(6))
        m8a, m8b = take(8), take(8)
        r_one = take(4)

        ps = ctx.enter_context(nc.psum_tensor("ps", [P, 8, HALF], F32))
        bank = {name: ps[:, n, :] for n, name in enumerate(BANKS)}

        full = {b: sem(f"{b}_full") for b in BANKS}
        free = {b: sem(f"{b}_free") for b in BANKS}
        passed = sem("passed")
        const_in = sem("const_in")
        tab_in = sem("tab_in")
        x_in = [sem(f"x_in{n}") for n in range(2)]
        k_stored = [sem(f"k_stored{n}") for n in range(2)]
        w_in = sem("w_in")
        wo_in, a_in, b_in = sem("wo_in"), sem("a_in"), sem("b_in")
        poles_T = sem("poles_T")
        dve1 = sem("dve1")
        arg_ready = sem("arg_ready")
        sin_done = sem("sin_done")
        exp_done = sem("exp_done")
        tabs_ready = sem("tabs_ready")
        xT_ready = sem("xT_ready")
        r_parts_ready = sem("r_parts_ready")
        d_parts_ready = sem("d_parts_ready")
        r_ready = sem("r_ready")
        d_ready = sem("d_ready")
        k_ready = sem("k_ready")
        krow_ready = sem("krow_ready")
        wmax = sem("wmax")
        wmax_all = sem("wmax_all")
        wscale = sem("wscale")
        w_scaled = sem("w_scaled")
        w_hi = sem("w_hi")
        w_lo = sem("w_lo")
        pool2 = sem("pool2")
        prep_full = sem("prep_full")
        prep_hi = sem("prep_hi")
        prep_free = sem("prep_free")
        keys_T = sem("keys_T")
        keys_Ts = sem("keys_Ts")
        blocks_zero = sem("blocks_zero")
        alibi_in = sem("alibi_in")
        h_loaded = sem("h_loaded")
        hres_loaded = sem("hres_loaded")
        out_stored = sem("out_stored")
        stats1, stats2 = sem("stats1"), sem("stats2")
        mv_ready = [sem("mean_var1"), sem("mean_var2")]
        rsd = [sem("rstd_steps1"), sem("rstd_steps2")]
        xn1_ready, xn2_ready = sem("xn1_ready"), sem("xn2_ready")
        hi_done = sem("hi_done")
        keys_copied = sem("keys_copied")
        max_ready = sem("max_ready")
        shifted = sem("shifted")
        exps_done = sem("exps_done")
        sums = sem("sums")
        probs_ready = sem("probs_ready")
        route = sem("route")
        route_exp = sem("route_exp")

        NPREP = 2 * KT + 1

        HI = [("x2_0", "ffn"), ("x2_1", "ffn"), ("zT", "ffn"), ("x1_0", "next"), ("x1_1", "next"),
              ("a_0", "attn"), ("a_1", "attn")]

        def hi_after(user, i):
            at = [u for u, _ in HI].index(user)
            if not isinstance(i, int):
                return (i - STEADY[0]) * len(HI) + hi_after(user, STEADY[0])
            return (sum(has(part, j) for j in range(FIRST, i) for _, part in HI)
                    + sum(has(part, i) for _, part in HI[:at + 1]))

        def filled(eng, user, i):
            wait(eng, full[BANK_OF[user]], uses_before(user, i) + 1)

        def emptied(eng, user, i):
            wait(eng, free[BANK_OF[user]], uses_before(user, i) + 1)

        def take_bank(eng, user, i):
            wait(eng, free[BANK_OF[user]], uses_before(user, i))

        def phase1_over(eng):
            eng.wait_ge(krow_ready, SEQ)
            for b in range(2):
                eng.wait_ge(k_stored[b], 64 * CHUNKS // 2)

        def apart(eng):
            eng.sem_inc(passed)

        block = ctx.enter_context(nc.Block())

        @block.sync
        def _(sp):
            for dst, src in ((ident[:, :], ident_c), (al_s, abslog), (ph_s, phase)):
                sp.dma_start(dst, src).then_inc(const_in, 16)
            for dst, src in ((times, times_c), (turns, turns_c)):
                sp.dma_start(dst, src).then_inc(tab_in, 16)
            sp.dma_start(keys_s[0:NE, :], keys).then_inc(const_in, 16)
            sp.dma_start(wq_s[:, :], wq).then_inc(const_in, 16)
            x_v = x.rearrange("c h n t -> c (h n t)")
            k_v = h_dram.rearrange("(c h) (qh ql r) -> ql c h qh r", h=SEQ, ql=2, r=RW_)

            def load_x(n, buf):
                w = HC * 2 * MODES
                sp.dma_start(xin[buf], x_v[:, bass.ds(n * w, w)]).then_inc(x_in[buf], 16)

            def store_k(n, buf, j):
                wait(sp, krow_ready, HC * (n + 1))
                src = krow[buf].rearrange("p (h q r) -> p h q r", h=HC, q=2)
                for ql in range(2):
                    for qh in range(2):
                        sp.dma_start(k_v[ql, :, bass.ds(n * HC, HC), qh, :],
                                     src[ql * BATCH:(ql + 1) * BATCH, :, qh, :]).then_inc(k_stored[buf], 16)

            load_x(0, 0)
            load_x(1, 1)
            sp.wait_ge(tabs_ready, 1)
            sp.dma_start(stage[:, :].rearrange("p (k n) -> p k n", k=KT),
                         wqkv.rearrange("(k p) n -> p k n", p=P)).then_inc(w_in, 16)
            with sp.Fori(0, CHUNKS // 2 - 1) as j:
                for b in range(2):
                    n = 2 * j + b
                    wait(sp, xT_ready, n + 1)
                    load_x(n + 2, b)
                    store_k(n, b, j)
            for b in range(2):
                store_k(CHUNKS - 2 + b, b, CHUNKS // 2 - 1)
            phase1_over(sp)
            sp.dma_start(alibi, alibi_c).then_inc(alibi_in, 16)

            def load(dst, tile, done):
                sp.dma_start(dst, h_dram[bass.ds(tile * P, P), :]).then_inc(done, 16)

            load(h_in, 0, h_loaded)

            def step(i, on):
                if on("next"):
                    if not isinstance(i, int) or i + 2 < TILES:
                        filled(sp, "x1_1", i)
                        load(h_in, i + 2, h_loaded)
                if on("ffn"):
                    emptied(sp, "f_0", i)
                    apart(sp)
                    emptied(sp, "f_1", i)
                    sp.dma_start(out[bass.ds((i - 2) * P, P), :], h_out).then_inc(out_stored, 16)
                if on("attn"):
                    if on("proj"):
                        emptied(sp, "o_0", i)
                        apart(sp)
                        emptied(sp, "o_1", i)
                    load(h_res, i, hres_loaded)

            steps(sp, step)
            sp.wait_ge(out_stored, 16 * TILES)

        @block.tensor
        def _(pe):
            eye = ident[:, :]
            pe.wait_ge(const_in, 16 * 5)
            for src, at in ((al_s, 0), (ph_s, 1)):
                for half in range(2):
                    mm = pe.matmul(ps[half * 64:half * 64 + 64, at, 0:SEQ], src, ident[0:SEQ, 0:SEQ],
                                   start=True, stop=True)
            mm.then_inc(poles_T, 1)
            pe.matmul(ps[0:RDIM, 2, 0:NE], keys_s[0:NE, :], ident[0:NE, 0:NE],
                      start=True, stop=True).then_inc(keys_T, 1)
            pe.wait_ge(tabs_ready, 1)

            def chunk_turn(n, j, b):
                pe.wait_ge(x_in[b], 16 * (j + 1))
                wait(pe, d_parts_ready, n - 1)
                apart(pe)
                v = xin[b].rearrange("c (h n t) -> c h t n", h=HC, t=2)
                for t in range(2):
                    for h in range(HC):
                        for half in range(2):
                            mm = pe.matmul(ps[half * 64:half * 64 + 64, b, (t * HC + h) * 64:(t * HC + h + 1) * 64],
                                           v[:, h, t, :], ident[0:BATCH, 0:BATCH], start=True, stop=True)
                mm.then_inc(xT_ready, 1)

            def chunk_contract(n, b):
                wait(pe, r_ready, n + 1)
                wait(pe, d_ready, n + 1)
                for h in range(HC):
                    wait(pe, krow_ready, HC * (n - 1) + h + 1)
                    for q in range(2):
                        mm = pe.matmul(ps[:, 4 + h, q * RW_:(q + 1) * RW_],
                                       d_full[b][:, h * DW_ + q * P:h * DW_ + (q + 1) * P],
                                       r_full[b][:, h * RW_:(h + 1) * RW_], start=True, stop=True)
                    mm.then_inc(k_ready, 1)

            for b in range(2):
                chunk_turn(b, 0, b)
            chunk_contract(0, 0)
            chunk_turn(2, 1, 0)
            chunk_contract(1, 1)
            chunk_turn(3, 1, 1)
            with pe.Fori(1, CHUNKS // 2 - 1) as j:
                for b in range(2):
                    chunk_contract(2 * j + b, b)
                    chunk_turn(2 * j + b + 2, j + 1, b)
            for b in range(2):
                chunk_contract(CHUNKS - 2 + b, b)
            pe.wait_ge(krow_ready, SEQ)

            PASSES = ((0, 0), (0, 1), (1, 0))

            def product(dst, xt, w, ktiles, cols):
                return product_part(dst, xt, w, ktiles, cols, 0, ktiles)

            def product_part(dst, xt, w, ktiles, cols, k0, k1):
                for k in range(k0, k1):
                    for n, (s, ws) in enumerate(PASSES):
                        mm = pe.matmul(dst, xt[:, s, k, :], w[:, ws, k, cols],
                                       start=(k == 0 and n == 0), stop=(k == ktiles - 1 and n == 2))
                return mm

            def fill(user, i, mm):
                mm.then_inc(full[BANK_OF[user]], 1)

            def turn(user, i, src, k0, nk):
                take_bank(pe, user, i)
                for k in range(nk):
                    mm = pe.transpose(bank[BANK_OF[user]][:, k * P:(k + 1) * P],
                                      src[:, (k0 + k) * P:(k0 + k + 1) * P], eye)
                fill(user, i, mm)

            def prepare_ffn_weights():
                n = 0
                pe.wait_ge(wscale, 4)
                take_bank(pe, "s_0", 2)
                for src, groups, per in ((0, KT, ZT), (ZT * HID, ZT, KT)):
                    for g in range(groups):
                        for part in range(per // 4):
                            wait(pe, prep_free, n)
                            for m in range(4):
                                mi = part * 4 + m
                                w = stage[:, src + mi * groups * P + g * P:src + mi * groups * P + (g + 1) * P]
                                mm = pe.transpose(bank["sc0"][:, m * P:(m + 1) * P], w, eye)
                            mm.then_inc(prep_full, 1)
                            n += 1
                pe.wait_ge(keys_Ts, 1)
                pe.wait_ge(prep_free, n)
                for k in range(KT):
                    mm = pe.matmul(bank["sc0"][:, k * NE:(k + 1) * NE], wq_s[:, k * P:(k + 1) * P], keysT_s[:, :],
                                   start=True, stop=True)
                mm.then_inc(prep_full, 1)
                pe.wait_ge(prep_free, NPREP)

            def step(i, on):
                if isinstance(i, int) and i == 0:
                    pe.wait_ge(w_lo, 1)
                    pe.wait_ge(blocks_zero, 1)
                if isinstance(i, int) and i == 2:
                    prepare_ffn_weights()
                if on("attn"):
                    emptied(pe, "x1_1", i - 1)
                    take_bank(pe, "kv", i)
                    fill("kv", i, product(bank["small"][:, 0:2 * DH], x1T, wqkv_s, KT, slice(HID, QKV)))
                if on("attn"):
                    take_bank(pe, "q_0", i)
                    fill("q_0", i, product(bank["wide0"], x1T, wqkv_s, KT, slice(0, HALF)))
                    wait(pe, keys_copied, i + 1)
                    turn("kT", i, k_rep, 0, 1)
                if on("ffn"):
                    wait(pe, xn2_ready, i - 1)
                    turn("x2_0", i, xn2, 0, 4)
                if on("attn"):
                    take_bank(pe, "q_1", i)
                    product_part(bank["wide1"], x1T, wqkv_s, KT, slice(HALF, HID), 0, 4)
                if on("ffn"):
                    turn("x2_1", i, xn2, 4, 4)
                if on("attn"):
                    fill("q_1", i, product_part(bank["wide1"], x1T, wqkv_s, KT, slice(HALF, HID), 4, KT))
                if on("ffn"):
                    emptied(pe, "x2_1", i)
                    take_bank(pe, "r", i)
                    fill("r", i, product(bank["small"][:, 0:NE], x2T, wr_s, KT, slice(0, NE)))
                    take_bank(pe, "z", i)
                    product_part(bank["wide0"], x2T, wa_s, KT, slice(0, BOT), 0, 3)
                if on("attn"):
                    emptied(pe, "q_0", i)
                    turn("qT_0", i, q_row, 0, 4)
                if on("ffn"):
                    product_part(bank["wide0"], x2T, wa_s, KT, slice(0, BOT), 3, 6)
                if on("attn"):
                    emptied(pe, "q_1", i)
                    turn("qT_1", i, q_row, 4, 4)
                if on("ffn"):
                    fill("z", i, product_part(bank["wide0"], x2T, wa_s, KT, slice(0, BOT), 6, KT))

                def scores(n):
                    take_bank(pe, f"s_{n}", i)
                    emptied(pe, f"qT_{n // 2}", i)
                    if n == 0:
                        emptied(pe, "kT", i)
                    for g in range(2):
                        for b in range(2):
                            mm = pe.matmul(bank[f"sc{n}"][b * 64:(b + 1) * 64, g * 256:(g + 1) * 256],
                                           qT[:, 2 * n + g, b * 64:(b + 1) * 64],
                                           k_blk[:, b, :, :].rearrange("p j k -> p (j k)"),
                                           start=True, stop=True)
                    fill(f"s_{n}", i, mm)

                if on("attn"):
                    scores(0)
                    scores(1)
                if on("ffn"):
                    emptied(pe, "z", i)
                    turn("zT", i, zg, 0, ZT)
                if on("attn"):
                    scores(2)
                    scores(3)
                if on("ffn"):
                    emptied(pe, "zT", i)
                    take_bank(pe, "f_0", i)
                    product_part(bank["wide1"], zT, wb_s, ZT, slice(0, HALF), 0, 2)
                if on("next"):
                    wait(pe, xn1_ready, i + 2)
                    turn("x1_0", i, xn1, 0, 4)
                if on("ffn"):
                    fill("f_0", i, product_part(bank["wide1"], zT, wb_s, ZT, slice(0, HALF), 2, ZT))
                    take_bank(pe, "f_1", i)
                    product_part(bank["wide0"], zT, wb_s, ZT, slice(HALF, HID), 0, 2)
                if on("next"):
                    turn("x1_1", i, xn1, 4, 4)
                if on("ffn"):
                    fill("f_1", i, product_part(bank["wide0"], zT, wb_s, ZT, slice(HALF, HID), 2, ZT))
                if on("proj"):
                    if isinstance(i, int) and i == 1:
                        pe.wait_ge(w_lo, 2)
                    emptied(pe, "a_1", i - 1)
                    take_bank(pe, "o_0", i)
                    fill("o_0", i, product(bank["wide1"], attT, wo_s, KT, slice(0, HALF)))
                    take_bank(pe, "o_1", i)
                    fill("o_1", i, product(bank["wide0"], attT, wo_s, KT, slice(HALF, HID)))
                if on("attn"):
                    for u in range(4):
                        wait(pe, probs_ready, 4 * i + u + 1)
                        take_bank(pe, f"p_{u}", i)
                        for m in range(4):
                            mm = pe.transpose(bank[f"sc{u}"][:, m * P:(m + 1) * P],
                                              probs[:, (4 * u + m) * P:(4 * u + m + 1) * P], eye)
                        fill(f"p_{u}", i, mm)
                    for u in range(4):
                        emptied(pe, f"p_{u}", i)
                        if u == 0:
                            emptied(pe, "kv", i)
                        for m in range(4):
                            pair = 4 * u + m
                            chunk = (pair // 2) % 4
                            for b in range(2):
                                mm = pe.matmul(bank[f"sc{u // 2}"][(pair % 2) * 64:(pair % 2) * 64 + 64,
                                                                   chunk * P + b * 64:chunk * P + (b + 1) * 64],
                                               v_blk[:, b, :], pT[:, pair, b * 64:(b + 1) * 64],
                                               start=True, stop=True)
                        if u % 2 == 1:
                            fill(f"a_{u // 2}", i, mm)

            steps(pe, step)

        @block.scalar
        def _(act):
            cp = ACT.Copy
            act.wait_ge(keys_T, 1)
            act.activation(keysT_s[:, :], ps[0:RDIM, 2, 0:NE], cp).then_inc(keys_Ts, 1)
            for v in range(2):
                act.wait_ge(arg_ready, v + 1)
                act.activation(vtab[v], vtab[v], ACT.Sin).then_inc(sin_done, 1)
            act.wait_ge(arg_ready, 3)
            act.activation(etab, etab, ACT.Exp).then_inc(exp_done, 1)

            def chunk(n, j, b):
                if not (isinstance(j, int) and j == 0):
                    act.wait_ge(k_stored[b], 64 * j)
                for h in range(HC):
                    wait(act, k_ready, HC * n + h + 1)
                    act.activation(krow[b][:, h * HALF:(h + 1) * HALF], ps[:, 4 + h, :], cp).then_inc(krow_ready, 1)

            def split_loaded(w, src, dst):
                act.wait_ge(wscale, w + 1)
                act.activation(src, src, cp, scale=scales[:, w, 4:5]).then_inc(w_scaled, 1)
                act.wait_ge(w_scaled, w + 1)
                act.activation(dst, src, cp).then_inc(w_hi, 1)

            for b in range(2):
                chunk(b, 0, b)
            with act.Fori(1, MID) as j:
                for b in range(2):
                    chunk(2 * j + b, j, b)
            split_loaded(QW, stage[:, :].rearrange("p (k n) -> p k n", k=KT), wqkv_s[:, 0, :, :])
            with act.Fori(MID, CHUNKS // 2) as j:
                for b in range(2):
                    chunk(2 * j + b, j, b)
            phase1_over(act)

            def prepare_ffn_weights():
                n = 0
                for w, groups, per, dst in ((AW, KT, ZT, wa_s), (BW, ZT, KT, wb_s)):
                    for g in range(groups):
                        for part in range(per // 4):
                            act.wait_ge(prep_full, n + 1)
                            act.activation(dst[:, 0, g, part * HALF:(part + 1) * HALF], bank["sc0"], cp,
                                           scale=scales[:, w, 4:5]).then_inc(prep_hi, 1)
                            n += 1
                act.wait_ge(wscale, 5)
                act.activation(wr_s[:, 0, :, :].rearrange("p k e -> p (k e)"), bank["sc0"], cp,
                               scale=scales[:, RW, 4:5]).then_inc(prep_hi, 1)

            def hi(user, i, dst):
                filled(act, user, i)
                act.activation(dst, bank[BANK_OF[user]], cp).then_inc(hi_done, 1)

            def evac(user, i, dst):
                filled(act, user, i)
                act.activation(dst, bank[BANK_OF[user]], cp).then_inc(free[BANK_OF[user]], 1)

            def halves(t, k0, nk):
                return t[:, 0, k0:k0 + nk, :].rearrange("p k t -> p (k t)")

            def step(i, on):
                if isinstance(i, int) and i == 2:
                    prepare_ffn_weights()
                if on("attn"):
                    filled(act, "kv", i)
                    act.activation(k_rep.rearrange("p (j d) -> p j d", j=4),
                                   bank["small"][:, 0:DH].unsqueeze(1).broadcast_to([P, 4, DH]),
                                   cp).then_inc(keys_copied, 1)
                    for b in range(2):
                        for m in range(2):
                            ins = act.activation(v_blk[m * 64:(m + 1) * 64, b, m * DH:(m + 1) * DH],
                                                 bank["small"][b * 64:(b + 1) * 64, DH:2 * DH], cp)
                    ins.then_inc(free["small"], 1)
                    evac("q_0", i, q_row[:, 0:HALF])
                    filled(act, "kT", i)
                    for j in range(4):
                        rows = slice(j * 32, j * 32 + 32)
                        ins = act.activation(k_blk[rows, :, j, :],
                                             bank["small"][rows, 0:P].rearrange("p (b k) -> p b k", b=2), cp)
                    ins.then_inc(free["small"], 1)
                if on("ffn"):
                    hi("x2_0", i, halves(x2T, 0, 4))
                    hi("x2_1", i, halves(x2T, 4, 4))
                if on("attn"):
                    evac("q_1", i, q_row[:, HALF:HID])
                    evac("qT_0", i, qT[:, 0:4, :].rearrange("p g t -> p (g t)"))
                if on("ffn"):
                    wait(act, route, 8 * (i - 2) + 6)
                    act.activation(r_exp, r_exp, ACT.Exp).then_inc(route_exp, 1)
                if on("attn"):
                    evac("qT_1", i, qT[:, 4:8, :].rearrange("p g t -> p (g t)"))
                if on("ffn"):
                    filled(act, "zT", i)
                    act.activation(halves(zT, 0, ZT), bank["turn"], cp).then_inc(hi_done, 1)
                if on("next"):
                    hi("x1_0", i, halves(x1T, 0, 4))
                    hi("x1_1", i, halves(x1T, 4, 4))
                if on("attn"):
                    for n in range(2):
                        wait(act, shifted, 2 * i + n + 1)
                        v = probs[:, n * 1024:(n + 1) * 1024]
                        act.activation(v, v, ACT.Exp).then_inc(exps_done, 1)
                    for u in range(4):
                        evac(f"p_{u}", i, pT[:, 4 * u:4 * u + 4, :].rearrange("p u t -> p (u t)"))
                    for u in range(2):
                        hi(f"a_{u}", i, halves(attT, 4 * u, 4))
                if isinstance(i, int) and i == 0:
                    split_loaded(OW, stage[:, 0:KT * HID].rearrange("p (k n) -> p k n", k=KT), wo_s[:, 0, :, :])

            steps(act, step)

        @block.gpsimd
        def _(pool):
            cnt = [0]

            def link(ins):
                cnt[0] += 1
                ins.then_inc(pool2, 1)
                pool.wait_ge(pool2, cnt[0])

            def scale_of_all(w):
                pool.wait_ge(wmax, w + 1)
                pool.partition_all_reduce(scales[:, w, 1:2], scales[:, w, 0:1], P, RMAX).then_inc(wmax_all, 1)

            def chunk(n, j, b):
                wait(pool, r_parts_ready, n + 1)
                wait(pool, k_ready, HC * (n - 1))
                pool.tensor_tensor(r_full[b], r_part[b][0], r_part[b][1], ALU.add).then_inc(r_ready, 1)
                wait(pool, d_parts_ready, n + 1)
                pool.tensor_tensor(d_full[b], d_part[b][0], d_part[b][1], ALU.add).then_inc(d_ready, 1)

            def lo_part(w, src, dst, hi_):
                pool.wait_ge(w_hi, w + 1)
                pool.tensor_tensor(dst, src, hi_, ALU.subtract).then_inc(w_lo, 1)

            for b in range(2):
                chunk(b, 0, b)
            with pool.Fori(1, MID) as j:
                for b in range(2):
                    chunk(2 * j + b, j, b)
            scale_of_all(QW)
            lo_part(QW, stage[:, :].rearrange("p (k n) -> p k n", k=KT), wqkv_s[:, 1, :, :], wqkv_s[:, 0, :, :])
            pool.wait_ge(w_lo, 1)
            pool.dma_start(stage[:, 0:KT * HID].rearrange("p (k n) -> p k n", k=KT),
                           wo.rearrange("(k p) n -> p k n", p=P)).then_inc(wo_in, 16)
            with pool.Fori(MID, CHUNKS // 2) as j:
                for b in range(2):
                    chunk(2 * j + b, j, b)
            phase1_over(pool)
            link(pool.memset(k_blk, 0.0))
            link(pool.memset(v_blk, 0.0))
            pool.memset(half_neg, -0.5).then_inc(blocks_zero, 1)
            pool.wait_ge(blocks_zero, 1)

            def rstd(l, n):
                done, v, base = rsd[l], rs[:, l, :], 6 * (n)
                wait(pool, mv_ready[l], n + 1)
                apart(pool)
                pool.tensor_scalar(v[:, 0:1], mv[:, l, 1:2], EPS, None, ALU.add).then_inc(done, 1)
                pool.wait_ge(done, base + 1)
                pool.tensor_tensor(v[:, 1:2], v[:, 0:1], half_neg, ALU.pow).then_inc(done, 1)
                pool.wait_ge(done, base + 2)
                pool.tensor_tensor(v[:, 2:3], v[:, 1:2], v[:, 1:2], ALU.mult).then_inc(done, 1)
                pool.wait_ge(done, base + 3)
                pool.tensor_tensor(v[:, 3:4], v[:, 2:3], v[:, 0:1], ALU.mult).then_inc(done, 1)
                pool.wait_ge(done, base + 4)
                apart(pool)
                pool.tensor_scalar(v[:, 4:5], v[:, 3:4], -0.5, 1.5, ALU.mult, ALU.add).then_inc(done, 1)
                pool.wait_ge(done, base + 5)
                pool.tensor_tensor(v[:, 5:6], v[:, 1:2], v[:, 4:5], ALU.mult).then_inc(done, 1)

            def step(i, on):
                if isinstance(i, int) and i == 2:
                    scale_of_all(RW)
                if on("next"):
                    rstd(0, i + 1)
                if on("proj"):
                    rstd(1, i - 1)
                if isinstance(i, int) and i == -1:
                    scale_of_all(OW)
                if isinstance(i, int) and i == 0:
                    lo_part(OW, stage[:, 0:KT * HID].rearrange("p (k n) -> p k n", k=KT),
                            wo_s[:, 1, :, :], wo_s[:, 0, :, :])
                    pool.wait_ge(w_lo, 2)
                    pool.dma_start(stage[:, 0:ZT * HID].rearrange("p (m k) -> p m k", m=ZT),
                                   aw.rearrange("(m p) k -> p m k", p=P)).then_inc(a_in, 16)
                    pool.dma_start(stage[:, ZT * HID:2 * ZT * HID].rearrange("p (m k) -> p m k", m=KT),
                                   bw.rearrange("(m p) k -> p m k", p=P)).then_inc(b_in, 16)
                if isinstance(i, int) and i == 1:
                    scale_of_all(AW)
                    scale_of_all(BW)

            steps(pool, step)

        @block.vector
        def _(dve):
            cnt = [0]

            def link(ins):
                cnt[0] += 1
                ins.then_inc(dve1, 1)
                dve.wait_ge(dve1, cnt[0])

            def wrap(dst, src, n_):
                link(dve.tensor_scalar(n_, src, 1 / (2 * math.pi), ROUND, ALU.mult, ALU.add))
                link(dve.tensor_scalar(n_, n_, ROUND, None, ALU.subtract))
                link(dve.scalar_tensor_tensor(dst, n_, -TWO_PI_HI, src, ALU.mult, ALU.add))
                link(dve.scalar_tensor_tensor(dst, n_, -TWO_PI_LO, dst, ALU.mult, ALU.add))

            dve.wait_ge(poles_T, 1)
            link(dve.tensor_copy(aT, ps[:, 0, 0:SEQ]))
            link(dve.tensor_copy(phT, ps[:, 1, 0:SEQ]))
            wrap(phT, phT, g4[:, 0, :])
            dve.wait_ge(tab_in, 32)
            tb = times.unsqueeze(1).broadcast_to([P, SEQ, TK])
            link(dve.tensor_tensor(th, phT.unsqueeze(2).broadcast_to([P, SEQ, TK]), tb, ALU.mult))
            wrap(th, th, turn_n)
            for v in range(2):
                link(dve.tensor_tensor(vtab[v], th, turns[:, v, :].unsqueeze(1).broadcast_to([P, SEQ, TK]), ALU.add))
                link(dve.tensor_scalar(turn_n, vtab[v], math.pi, -2 * math.pi, ALU.is_gt, ALU.mult))
                link(dve.tensor_tensor(vtab[v], vtab[v], turn_n, ALU.add))
                dve.tensor_scalar(vtab[v], vtab[v], PI_SAFE, -PI_SAFE, ALU.min, ALU.max).then_inc(arg_ready, 1)
            dve.tensor_tensor(etab, aT.unsqueeze(2).broadcast_to([P, SEQ, TK]), tb, ALU.mult).then_inc(arg_ready, 1)
            dve.wait_ge(exp_done, 1)
            dve.wait_ge(sin_done, 2)
            for v in range(2):
                link(dve.tensor_tensor(vtab[v], vtab[v], etab, ALU.mult))
            re, im, den, t0, t1, gre, gim, t2 = (g4[:, k, :] for k in range(8))
            one = NA + 1
            link(dve.tensor_scalar(re, vtab[0][:, :, one], -1.0, None, ALU.add))
            link(dve.tensor_copy(im, vtab[1][:, :, one]))
            link(dve.tensor_tensor(den, aT, aT, ALU.mult))
            link(dve.tensor_tensor(t0, phT, phT, ALU.mult))
            link(dve.tensor_tensor(den, den, t0, ALU.add))
            link(dve.reciprocal(t2, den))
            link(dve.tensor_tensor(t0, re, aT, ALU.mult))
            link(dve.tensor_tensor(t1, im, phT, ALU.mult))
            link(dve.tensor_tensor(gre, t0, t1, ALU.add))
            link(dve.scalar_tensor_tensor(gre, gre, 2.0, t2, ALU.mult, ALU.mult))
            link(dve.tensor_tensor(t0, im, aT, ALU.mult))
            link(dve.tensor_tensor(t1, re, phT, ALU.mult))
            link(dve.tensor_tensor(gim, t0, t1, ALU.subtract))
            link(dve.scalar_tensor_tensor(gim, gim, 2.0, t2, ALU.mult, ALU.mult))
            s1, s2 = (vtab[v][:, :, NA + NB:TK] for v in range(2))
            grb, gib = (g.unsqueeze(2).broadcast_to([P, SEQ, NQ]) for g in (gre, gim))
            tmp = th[:, :, 0:NQ]
            link(dve.tensor_tensor(gtab[0], s1, grb, ALU.mult))
            link(dve.tensor_tensor(tmp, s2, gib, ALU.mult))
            link(dve.tensor_tensor(gtab[0], gtab[0], tmp, ALU.add))
            link(dve.tensor_tensor(gtab[1], s2, grb, ALU.mult))
            link(dve.tensor_tensor(tmp, s1, gib, ALU.mult))
            dve.tensor_tensor(gtab[1], gtab[1], tmp, ALU.subtract).then_inc(tabs_ready, 1)
            dve.wait_ge(tabs_ready, 1)

            def chunk(n, j, b):
                hs = bass.ds(n * HC, HC)
                wait(dve, r_ready, n - 1)
                for v in range(2):
                    alpha = vtab[v][:, hs, 0:NA].unsqueeze(3).broadcast_to([P, HC, NA, NB])
                    beta = vtab[v][:, hs, NA:NA + NB].unsqueeze(2).broadcast_to([P, HC, NA, NB])
                    ins = dve.tensor_tensor(r_part[b][v].rearrange("p (h a b) -> p h a b", h=HC, a=NA),
                                            alpha, beta, ALU.mult)
                ins.then_inc(r_parts_ready, 1)
                wait(dve, d_ready, n - 1)
                wait(dve, xT_ready, n + 1)
                for v in range(2):
                    xs = ps[:, b, v * HC * 64:(v + 1) * HC * 64].rearrange("p (h c) -> p h c", h=HC)
                    ins = dve.tensor_tensor(d_part[b][v].rearrange("p (h q c) -> p h q c", h=HC, q=NQ),
                                            xs.unsqueeze(2).broadcast_to([P, HC, NQ, BATCH]),
                                            gtab[v][:, hs, :].unsqueeze(3).broadcast_to([P, HC, NQ, BATCH]), ALU.mult)
                ins.then_inc(d_parts_ready, 1)

            def weight_max(w, view):
                dve.tensor_reduce(scales[:, w, 0:1], view, AX, ALU.max, apply_absolute_value=True).then_inc(wmax, 1)

            def weight_scale(w):
                dve.wait_ge(wmax_all, w + 1)
                link(dve.tensor_scalar(scales[:, w, 1:2], scales[:, w, 1:2], 1e-30, None, ALU.max))
                link(dve.tensor_scalar(scales[:, w, 2:3].bitcast(I32), scales[:, w, 1:2].bitcast(I32),
                                       0x7F800000, None, ALU.bitwise_and))
                link(dve.reciprocal(scales[:, w, 3:4], scales[:, w, 2:3]))
                link(dve.tensor_scalar(scales[:, w, 5:6], scales[:, w, 2:3], 0.125, None, ALU.mult))
                dve.tensor_scalar(scales[:, w, 4:5], scales[:, w, 3:4], 8.0, None, ALU.mult).then_inc(wscale, 1)
                dve.wait_ge(wscale, w + 1)

            for b in range(2):
                chunk(b, 0, b)
            with dve.Fori(1, MID) as j:
                for b in range(2):
                    chunk(2 * j + b, j, b)
            dve.wait_ge(w_in, 16)
            weight_max(QW, stage[:, :])
            weight_scale(QW)
            with dve.Fori(MID, CHUNKS // 2) as j:
                for b in range(2):
                    chunk(2 * j + b, j, b)
            phase1_over(dve)
            inv = [scales[:, w, 5:6] for w in range(5)]
            c_score, c_proj, c_ffn = (consts[:, k:k + 1] for k in range(3))
            link(dve.scalar_tensor_tensor(c_score, inv[QW], SOFT_SCALE, inv[QW], ALU.mult, ALU.mult))

            def prepare_ffn_weights():
                n = 0
                for w, groups, per, dst in ((AW, KT, ZT, wa_s), (BW, ZT, KT, wb_s)):
                    for g in range(groups):
                        for part in range(per // 4):
                            cols = slice(part * HALF, (part + 1) * HALF)
                            dve.wait_ge(prep_hi, n + 1)
                            dve.scalar_tensor_tensor(dst[:, 1, g, cols], bank["sc0"], scales[:, w, 4:5],
                                                     dst[:, 0, g, cols], ALU.mult, ALU.subtract).then_inc(prep_free, 1)
                            n += 1
                dve.wait_ge(prep_full, NPREP)
                weight_max(RW, bank["sc0"])
                weight_scale(RW)
                dve.wait_ge(prep_hi, NPREP)
                dve.scalar_tensor_tensor(wr_s[:, 1, :, :].rearrange("p k e -> p (k e)"), bank["sc0"], scales[:, RW, 4:5],
                                         wr_s[:, 0, :, :].rearrange("p k e -> p (k e)"),
                                         ALU.mult, ALU.subtract).then_inc(prep_free, 1)

            def lo(user, i, t, k0, nk):
                wait(dve, hi_done, hi_after(user, i))
                dve.tensor_tensor(t[:, 1, k0:k0 + nk, :].rearrange("p k t -> p (k t)"), bank[BANK_OF[user]],
                                  t[:, 0, k0:k0 + nk, :].rearrange("p k t -> p (k t)"),
                                  ALU.subtract).then_inc(free[BANK_OF[user]], 1)

            def norm_stats(l, src, n):
                for k in range(2):
                    dve.bn_stats(bn[:, l, 6 * k:6 * k + 6], src[:, k * HALF:(k + 1) * HALF]).then_inc(stats1, 1)
                wait(dve, stats1, 2 * (n + 1))
                apart(dve)
                dve.bn_aggr(mv[:, l, :], bn[:, l, :]).then_inc(mv_ready[l], 1)

            def normalise(l, src, dst, n, done):
                wait(dve, rsd[l], 6 * (n + 1))
                dve.tensor_scalar(dst, src, mv[:, l, 0:1], rs[:, l, 5:6], ALU.subtract, ALU.mult).then_inc(done, 1)

            def step(i, on):
                if isinstance(i, int) and i == 2:
                    prepare_ffn_weights()
                if on("next"):
                    wait(dve, h_loaded, 16 * (i + 2))
                    norm_stats(0, h_in, i + 1)
                if on("ffn"):
                    lo("x2_0", i, x2T, 0, 4)
                    lo("x2_1", i, x2T, 4, 4)
                if on("next"):
                    normalise(0, h_in, xn1, i + 1, xn1_ready)
                if on("ffn"):
                    t = i - 2
                    filled(dve, "r", i)
                    base = 8 * t
                    dve.tensor_scalar(r_sc, bank["small"][:, 0:NE], inv[RW], None, ALU.mult).then_inc(free["small"], 1)
                    emptied(dve, "r", i)
                    apart(dve)
                    dve.max(m8a, r_sc).then_inc(route, 1)
                    wait(dve, route, base + 1)
                    apart(dve)
                    dve.match_replace(r_w1, m8a, r_sc, TAKEN).then_inc(route, 1)
                    wait(dve, route, base + 2)
                    apart(dve)
                    dve.max(m8b, r_w1).then_inc(route, 1)
                    wait(dve, route, base + 3)
                    apart(dve)
                    dve.match_replace(r_w2, m8b, r_w1, TAKEN).then_inc(route, 1)
                    wait(dve, route, base + 4)
                    dve.tensor_scalar(r_sel, r_w2, TAKEN, None, ALU.is_equal).then_inc(route, 1)
                    dve.tensor_scalar(r_exp, r_sc, m8a[:, 0:1], None, ALU.subtract).then_inc(route, 1)
                    wait(dve, route_exp, t + 1)
                    dve.scalar_tensor_tensor(r_gate, r_exp, 1.0, r_sel, ALU.mult, ALU.mult,
                                             accum_out=r_one[:, 0:1]).then_inc(route, 1)
                    wait(dve, route, base + 7)
                    dve.reciprocal(r_one[:, 1:2], r_one[:, 0:1]).then_inc(route, 1)
                    wait(dve, route, base + 8)
                    filled(dve, "z", i)
                    dve.scalar_tensor_tensor(zg.rearrange("p (e r) -> p e r", r=RANK),
                                             bank["wide0"].rearrange("p (e r) -> p e r", r=RANK), r_one[:, 1:2],
                                             r_gate.unsqueeze(2).broadcast_to([P, NE, RANK]),
                                             ALU.mult, ALU.mult).then_inc(free["wide0"], 1)

                def biased(n):
                    filled(dve, f"s_{n}", i)
                    cols = slice(n * HALF, (n + 1) * HALF)
                    dve.scalar_tensor_tensor(probs[:, cols], bank[f"sc{n}"], c_score, alibi[:, cols],
                                             ALU.mult, ALU.add).then_inc(free[f"sc{n}"], 1)

                if on("attn"):
                    if isinstance(i, int) and i == 0:
                        dve.wait_ge(alibi_in, 16)
                    biased(0)
                    biased(1)
                if on("ffn"):
                    lo("zT", i, zT, 0, ZT)
                if on("attn"):
                    biased(2)
                    biased(3)
                p3 = probs.rearrange("p (h k) -> p h k", h=HEADS)
                if on("attn"):
                    emptied(dve, "s_3", i)
                    dve.tensor_reduce(smax, p3, AX, ALU.max).then_inc(max_ready, 1)
                if on("next"):
                    lo("x1_0", i, x1T, 0, 4)

                def result(n, user):
                    filled(dve, user, i)
                    cols = slice(n * HALF, (n + 1) * HALF)
                    dve.scalar_tensor_tensor(h_out[:, cols], bank[BANK_OF[user]], c_ffn, h_mid[:, cols],
                                             ALU.mult, ALU.add).then_inc(free[BANK_OF[user]], 1)

                if on("ffn"):
                    wait(dve, out_stored, 16 * (i - 2))
                    result(0, "f_0")
                if on("attn"):
                    wait(dve, max_ready, i + 1)
                    for n in range(2):
                        hh = slice(n * 16, (n + 1) * 16)
                        dve.tensor_tensor(p3[:, hh, :], p3[:, hh, :],
                                          smax[:, hh].unsqueeze(2).broadcast_to([P, 16, SEQ]),
                                          ALU.subtract).then_inc(shifted, 1)
                if on("next"):
                    lo("x1_1", i, x1T, 4, 4)
                if on("ffn"):
                    result(1, "f_1")
                if on("attn"):
                    wait(dve, exps_done, 2 * (i + 1))
                    dve.tensor_reduce(ssum, p3, AX, ALU.add).then_inc(sums, 1)
                    wait(dve, sums, 2 * i + 1)
                    dve.reciprocal(srec, ssum).then_inc(sums, 1)
                    wait(dve, sums, 2 * i + 2)
                    for n in range(4):
                        hh = slice(n * 8, (n + 1) * 8)
                        dve.tensor_tensor(p3[:, hh, :], p3[:, hh, :],
                                          srec[:, hh].unsqueeze(2).broadcast_to([P, 8, SEQ]),
                                          ALU.mult).then_inc(probs_ready, 1)
                if on("proj"):
                    wait(dve, hres_loaded, 16 * i)
                    for n, user in ((0, "o_0"), (1, "o_1")):
                        filled(dve, user, i)
                        cols = slice(n * HALF, (n + 1) * HALF)
                        dve.scalar_tensor_tensor(h_mid[:, cols], bank[BANK_OF[user]], c_proj, h_res[:, cols],
                                                 ALU.mult, ALU.add).then_inc(free[BANK_OF[user]], 1)
                        emptied(dve, user, i)
                        dve.bn_stats(bn[:, 1, 6 * n:6 * n + 6], h_mid[:, cols]).then_inc(stats2, 1)
                    wait(dve, stats2, 2 * i)
                    apart(dve)
                    dve.bn_aggr(mv[:, 1, :], bn[:, 1, :]).then_inc(mv_ready[1], 1)
                if on("attn"):
                    lo("a_0", i, attT, 0, 4)
                    lo("a_1", i, attT, 4, 4)
                if on("proj"):
                    normalise(1, h_mid, xn2, i - 1, xn2_ready)
                if isinstance(i, int) and i == -1:
                    dve.wait_ge(wo_in, 16)
                    weight_max(OW, stage[:, 0:KT * HID])
                    weight_scale(OW)
                    link(dve.tensor_tensor(c_proj, inv[QW], inv[OW], ALU.mult))
                if isinstance(i, int) and i == 1:
                    dve.wait_ge(a_in, 16)
                    dve.wait_ge(b_in, 16)
                    weight_max(AW, stage[:, 0:ZT * HID])
                    weight_max(BW, stage[:, ZT * HID:2 * ZT * HID])
                    weight_scale(AW)
                    weight_scale(BW)
                    link(dve.scalar_tensor_tensor(c_ffn, inv[AW], FFN_SCALE, inv[BW], ALU.mult, ALU.mult))

            steps(dve, step)


def _slopes(n):
    base = 2.0 ** (-2.0 ** (-(math.log2(n) - 3)))
    return (base ** np.arange(1, n + 1, dtype=np.float64)).astype(np.float32)


def _constants():
    ident = np.eye(P, dtype=np.float32)
    pos = np.arange(SEQ)
    bias = _slopes(HEADS)[None, :, None] * (pos[None, None, :] - pos[:, None, None]).astype(np.float32)
    bias = np.where(pos[None, None, :] <= pos[:, None, None], bias, np.float32(-1e30)).astype(np.float32)
    alibi = np.concatenate([bias, bias]).reshape(P, HEADS * SEQ)
    times = np.concatenate([NB * np.arange(NA), np.arange(NB), NA * NB * np.arange(NQ)]).astype(np.float32)
    times = np.ascontiguousarray(np.broadcast_to(times, (P, TK)))
    q = math.pi / 2
    offs = {0: ((q, 2 * q), (q, q), (q, 0)), 1: ((2 * q, 3 * q), (0, 0), (2 * q, q))}
    turns = np.zeros((P, 2, TK), np.float32)
    for v, groups in offs.items():
        at = 0
        for (re, im), n in zip(groups, (NA, NB, NQ)):
            turns[:MODES, v, at:at + n] = re
            turns[MODES:, v, at:at + n] = im
            at += n
    return {"ident": ident, "alibi": alibi, "times": times, "turns": turns}


_INS = ["x", "L0_tok_A_abslog", "L0_tok_A_phase", "L0_attn_Wqkv", "L0_attn_Wo",
        "L0_ffn_A_w", "L0_ffn_B_w", "L0_ffn_Wq_w", "L0_ffn_keys"]


def kernel(**inputs):
    import concourse.bacc as bacc
    from concourse.bass_utils import run_bass_kernel_spmd

    nc = bacc.Bacc("TRN2", target_bir_lowering=False, num_devices=1)
    arrays, args = {}, []
    for name, a in [(n, inputs[n]) for n in _INS] + list(_constants().items()):
        a = np.ascontiguousarray(a)
        arrays[f"in_{name}"] = a
        args.append(nc.dram_tensor(f"in_{name}", a.shape, mybir.dt.from_np(a.dtype), kind="ExternalInput").ap())
    out = nc.dram_tensor("out_rows", [BATCH * SEQ, HID], F32, kind="ExternalOutput").ap()
    vit_layer(nc, *args, out)
    r = run_bass_kernel_spmd(nc, [arrays], core_ids=[0])
    return r.results[0]["out_rows"].reshape(BATCH, SEQ, HID)
```

```python
import math
from contextlib import ExitStack

import numpy as np

import concourse.bass as bass
from concourse import mybir

F32 = mybir.dt.float32
F16 = mybir.dt.float16
I32 = mybir.dt.int32
ALU = mybir.AluOpType
ACT = mybir.ActivationFunctionType
AX = mybir.AxisListType.X
RMAX = bass.bass_isa.ReduceOp.max

P = 128
BATCH, SEQ, HID = 64, 64, 1024
MODES = 64
HEADS, DH = 32, 32
NE, RANK, TOPK, RDIM = 64, 8, 16, 16
BOT = NE * RANK
KT = HID // P
ZT = BOT // P
WO_PARTS = 4
TILES = BATCH * SEQ // P
EPS = 1e-5
SOFT_SCALE = DH ** -0.5
FFN_SCALE = 32 / TOPK
HALF = 512

NQ, NA, NB = 4, 16, 16
TK = NA + NB + NQ
HC = 4
CHUNKS = SEQ // HC
A_COLS, Q_COLS, B_COLS = slice(0, NA), slice(NA, NA + NQ), slice(NA + NQ, TK)
ROUND = 12582912.0
ROUND_13 = 1536.0
TWO_PI_HI = 6.28125
TWO_PI_LO = 2 * math.pi - TWO_PI_HI
TURN = 6.283185
TAKEN = -3.0e38

FIRST, LAST = -1, TILES + 1
STEADY = (3, TILES - 2)


def has(part, i):
    lo, hi = {"next": (-1, TILES - 2), "attn": (0, TILES - 1), "proj": (1, TILES), "ffn": (2, TILES + 1)}[part]
    return lo <= i <= hi


BANKS = {
    "turn": [("x2_0", "ffn"), ("x2_1", "ffn"), ("qT_0", "attn"), ("qT_1", "attn"),
             ("zT", "ffn"), ("x1_0", "next"), ("x1_1", "next")],
    "wide0": [("q_0", "attn"), ("z", "ffn"), ("f_1", "ffn"), ("o_1", "proj")],
    "wide1": [("q_1", "attn"), ("f_0", "ffn"), ("o_0", "proj")],
    "small": [("kv", "attn"), ("kT", "attn"), ("r", "ffn")],
    "sc0": [("s_0", "attn"), ("p_0", "attn"), ("a_0", "attn")],
    "sc1": [("s_1", "attn"), ("p_1", "attn"), ("a_1", "attn")],
    "sc2": [("s_2", "attn"), ("p_2", "attn")],
    "sc3": [("s_3", "attn"), ("p_3", "attn")],
}
BANK_OF = {user: bank for bank, users in BANKS.items() for user, _ in users}


def uses_before(user, i):
    users = BANKS[BANK_OF[user]]
    at = [u for u, _ in users].index(user)
    if not isinstance(i, int):
        return (i - STEADY[0]) * len(users) + uses_before(user, STEADY[0])
    return (sum(has(part, j) for j in range(FIRST, i) for _, part in users)
            + sum(has(part, i) for _, part in users[:at]))


def wait(eng, sem, value):
    if isinstance(value, int) and value <= 0:
        return
    eng.wait_ge(sem, value)


def steps(eng, body):
    for i in range(FIRST, STEADY[0]):
        body(i, lambda part, i=i: has(part, i))
    with eng.Fori(STEADY[0], STEADY[1]) as i:
        body(i, lambda part: True)
    for i in range(STEADY[1], LAST + 1):
        body(i, lambda part, i=i: has(part, i))


def vit_layer(nc, x, abslog, phase, wqkv, wo, aw, bw, wq, keys,
              ident_c, alibi_c, times_c, out):
    ctx = ExitStack()
    with ctx:
        def sb(name, shape, dt=F32):
            return ctx.enter_context(nc.sbuf_tensor(name, shape, dt))

        def sem(name):
            return ctx.enter_context(nc.semaphore(name))

        h_dram = nc.dram_tensor("h_rows", [BATCH * SEQ, HID], F32, kind="Internal").ap()

        QKV = HID + 2 * DH
        wqkv_s = sb("wqkv_s", [P, 2, KT, QKV], F16)
        wa_s = sb("wa_s", [P, 2, KT, BOT], F16)
        wr_s = sb("wr_s", [P, 2, KT, NE], F16)
        wb_s = sb("wb_s", [P, 2, ZT, HID], F16)
        wo_s = sb("wo_s", [P, 2, KT, HID], F16)
        stage = sb("stage", [P, KT * QKV])
        stage_a = wb_s[:, :, :, :].rearrange("p s k n -> p (s k n)").bitcast(F32)
        ident = sb("ident", [P, P])
        scales = sb("scales", [P, 5, 8])
        consts = sb("consts", [P, 8])
        keys_s = sb("keys_s", [P, RDIM])
        keysT_s = sb("keysT_s", [RDIM, NE])
        wq_s = sb("wq_s", [RDIM, HID])
        RW, QW, AW, OW, BW = range(5)

        ARENA = 17600
        arena = sb("arena", [P, ARENA])
        top = [0]

        def take(cols, dt=F32, rows=P):
            at = top[0]
            n = cols if dt == F32 else (cols + 1) // 2
            top[0] += n
            assert top[0] <= ARENA, top[0]
            v = arena[0:rows, at:at + n]
            return v if dt == F32 else v.bitcast(dt)

        al_s, ph_s = take(MODES, rows=SEQ), take(MODES, rows=SEQ)
        xin = [take(HC * 2 * MODES, rows=BATCH) for _ in range(2)]
        aT, phT = take(SEQ), take(SEQ)
        g4 = take(9 * SEQ).rearrange("p (k h) -> p k h", k=9)
        units = take(2 * SEQ).rearrange("p (m h) -> p m h", m=2)
        times = take(2 * TK).rearrange("p (v k) -> p v k", v=2)
        quarter = take(2)
        vtab = [take(SEQ * TK).rearrange("p (h k) -> p h k", k=TK) for _ in range(2)]
        gtab = [take(SEQ * NQ).rearrange("p (h q) -> p h q", q=NQ) for _ in range(2)]
        RW_ = NA * NB
        DW_ = NQ * BATCH
        at_parts = top[0]
        r_full, d_full = ([take(HC * RW_) for _ in range(2)] for _ in range(2))
        r_term, d_term = take(HC * RW_), take(HC * DW_)
        krow = [take(HC * HALF) for _ in range(2)]
        top[0] = at_parts
        turn, turn_abs, etab = (take(SEQ * TK).rearrange("p (h k) -> p h k", k=TK) for _ in range(3))

        top[0] = 0
        h_in = take(HID)
        h_res = take(HID)
        h_mid = take(HID)
        h_out = take(HID)
        xn1, xn2 = h_in, take(HID)
        x1T = take(2 * HID, F16).rearrange("p (s k t) -> p s k t", s=2, k=KT)
        x2T = take(2 * HID, F16).rearrange("p (s k t) -> p s k t", s=2, k=KT)
        attT = take(2 * HID, F16).rearrange("p (s k t) -> p s k t", s=2, k=KT)
        zT = take(2 * BOT, F16).rearrange("p (s k t) -> p s k t", s=2, k=ZT)
        q_then_p = take(HEADS * SEQ)
        q_row = q_then_p[:, 0:HID]
        qT = q_then_p[:, HID:2 * HID].bitcast(F16).rearrange("p (s g t) -> p s g t", s=2, g=KT)
        pT = q_then_p.rearrange("p (u t) -> p u t", t=P)
        k_rep = take(4 * DH)
        k_blk = take(2 * 2 * 4 * SEQ, F16).rearrange("p (s b j k) -> p s b j k", s=2, b=2, j=4)
        v_blk = take(2 * 2 * DH).rearrange("p (b m) -> p b m", b=2)
        probs = take(HEADS * SEQ)
        alibi = take(HEADS * SEQ)
        smax, ssum, srec = take(HEADS), take(HEADS), take(HEADS)
        zg = take(BOT)
        bn = take(24).rearrange("p (l k) -> p l k", l=2)
        mv = take(4).rearrange("p (l k) -> p l k", l=2)
        rs = take(16).rearrange("p (l k) -> p l k", l=2)
        half_neg = take(1)
        r_sc, r_w1, r_w2, r_sel, r_exp, r_gate = (take(NE) for _ in range(6))
        m8a, m8b = take(8), take(8)
        r_one = take(4)

        ps = ctx.enter_context(nc.psum_tensor("ps", [P, 8, HALF], F32))
        bank = {name: ps[:, n, :] for n, name in enumerate(BANKS)}

        full = {b: sem(f"{b}_full") for b in BANKS}
        free = {b: sem(f"{b}_free") for b in BANKS}
        passed = sem("passed")
        const_in = sem("const_in")
        tab_in = sem("tab_in")
        x_in = [sem(f"x_in{n}") for n in range(2)]
        k_stored = [sem(f"k_stored{n}") for n in range(2)]
        wqkv_in, wo_in, a_in, b_in = sem("wqkv_in"), sem("wo_in"), sem("a_in"), sem("b_in")
        poles_T = sem("poles_T")
        dve_steps = sem("dve_steps")
        poles_copied = sem("poles_copied")
        exponent_ready = sem("exponent_ready")
        turn_ready = sem("turn_ready")
        quarter_set = sem("quarter_set")
        pole_read = sem("pole_read")
        poles_inverse = sem("poles_inverse")
        g_ready = sem("g_ready")
        sin_done = sem("sin_done")
        exp_done = sem("exp_done")
        tabs_ready = sem("tabs_ready")
        xT_ready = sem("xT_ready")
        r_parts_ready = sem("r_parts_ready")
        d_parts_ready = sem("d_parts_ready")
        r_ready = sem("r_ready")
        d_ready = sem("d_ready")
        k_ready = sem("k_ready")
        krow_ready = sem("krow_ready")
        wmax = sem("wmax")
        wmax_all = sem("wmax_all")
        wscale = sem("wscale")
        wqkv_hi, wqkv_lo = sem("wqkv_hi"), sem("wqkv_lo")
        wo_hi, wo_lo = sem("wo_hi"), sem("wo_lo")
        router_filled, router_hi, router_lo = sem("router_filled"), sem("router_hi"), sem("router_lo")
        pool_steps = sem("pool_steps")
        prep_full = sem("prep_full")
        prep_hi = sem("prep_hi")
        prep_free = sem("prep_free")
        keys_T = sem("keys_T")
        keys_Ts = sem("keys_Ts")
        blocks_zero = sem("blocks_zero")
        alibi_in = sem("alibi_in")
        h_loaded = sem("h_loaded")
        hres_loaded = sem("hres_loaded")
        out_stored = sem("out_stored")
        stats1, stats2 = sem("stats1"), sem("stats2")
        mv_ready = [sem("mean_var1"), sem("mean_var2")]
        rsd = [sem("rstd_steps1"), sem("rstd_steps2")]
        xn1_ready, xn2_ready = sem("xn1_ready"), sem("xn2_ready")
        hi_done = sem("hi_done")
        keys_copied = sem("keys_copied")
        keys_hi = sem("keys_hi")
        max_ready = sem("max_ready")
        shifted = sem("shifted")
        exps_done = sem("exps_done")
        sums = sem("sums")
        probs_ready = sem("probs_ready")
        route = sem("route")
        route_exp = sem("route_exp")

        PREPS = [(AW, g, 0) for g in range(KT)] + [(BW, g, part) for g in range(ZT) for part in range(HID // HALF)]

        def ffn_weight(w):
            if w == AW:
                return stage_a.rearrange("p (m k) -> p m k", m=ZT), wa_s
            return stage[:, 0:ZT * HID].rearrange("p (m k) -> p m k", m=KT), wb_s

        HI = [("x2_0", "ffn"), ("x2_1", "ffn"), ("qT_0", "attn"), ("qT_1", "attn"), ("zT", "ffn"), ("x1_0", "next"), ("x1_1", "next"),
              ("a_0", "attn"), ("a_1", "attn")]

        def hi_after(user, i):
            at = [u for u, _ in HI].index(user)
            if not isinstance(i, int):
                return (i - STEADY[0]) * len(HI) + hi_after(user, STEADY[0])
            return (sum(has(part, j) for j in range(FIRST, i) for _, part in HI)
                    + sum(has(part, i) for _, part in HI[:at + 1]))

        def filled(eng, user, i):
            wait(eng, full[BANK_OF[user]], uses_before(user, i) + 1)

        def emptied(eng, user, i):
            wait(eng, free[BANK_OF[user]], uses_before(user, i) + 1)

        def take_bank(eng, user, i):
            wait(eng, free[BANK_OF[user]], uses_before(user, i))

        def phase1_over(eng):
            eng.wait_ge(krow_ready, SEQ)
            for b in range(2):
                eng.wait_ge(k_stored[b], 64 * CHUNKS // 2)

        def apart(eng):
            eng.sem_inc(passed)

        block = ctx.enter_context(nc.Block())

        @block.sync
        def _(sp):
            for dst, src in ((ident[:, :], ident_c), (al_s, abslog), (ph_s, phase)):
                sp.dma_start(dst, src).then_inc(const_in, 16)
            sp.dma_start(times, times_c).then_inc(tab_in, 16)
            sp.dma_start(keys_s[0:NE, :], keys).then_inc(const_in, 16)
            sp.dma_start(wq_s[:, :], wq).then_inc(const_in, 16)
            x_v = x.rearrange("c h n t -> c (h n t)")

            def load_x(n, buf):
                w = HC * 2 * MODES
                sp.dma_start(xin[buf], x_v[:, bass.ds(n * w, w)]).then_inc(x_in[buf], 16)

            load_x(0, 0)
            load_x(1, 1)
            sp.dma_start(stage[:, :].rearrange("p (k n) -> p k n", k=KT),
                         wqkv.rearrange("(k p) n -> p k n", p=P)).then_inc(wqkv_in, 16)
            sp.dma_start(stage_a.rearrange("p (m k) -> p m k", m=ZT),
                         aw.rearrange("(m p) k -> p m k", p=P)).then_inc(a_in, 16)

            def next_x(n, b):
                wait(sp, xT_ready, n + 1)
                load_x(n + 2, b)

            k_v = h_dram.rearrange("(c h) (qh ql r) -> ql c h qh r", h=SEQ, ql=2, r=RW_)

            def store_k(n, b):
                wait(sp, krow_ready, HC * (n + 1))
                src = krow[b].rearrange("p (h q r) -> p h q r", h=HC, q=2)
                for ql in range(2):
                    for qh in range(2):
                        sp.dma_start(k_v[ql, :, bass.ds(n * HC, HC), qh, :],
                                     src[ql * BATCH:(ql + 1) * BATCH, :, qh, :]).then_inc(k_stored[b], 16)

            next_x(0, 0)
            for n in range(1, 6):
                next_x(n, n % 2)
                store_k(n - 1, (n - 1) % 2)
            with sp.Fori(3, 3 + KT // 2) as j:
                for b in range(2):
                    n = 2 * j + b
                    next_x(n, b)
                    store_k(n - 1, 1 - b)
                    wait(sp, wqkv_lo, n - 5)
                    sp.dma_start(stage[:, bass.ds((n - 6) * HID, HID)],
                                 wo[bass.ds((n - 6) * P, P), :]).then_inc(wo_in, 16)
            for n in range(6 + KT, CHUNKS):
                store_k(n - 1, (n - 1) % 2)
            store_k(CHUNKS - 1, 1)
            phase1_over(sp)

            def load(dst, tile, done):
                sp.dma_start(dst, h_dram[bass.ds(tile * P, P), :]).then_inc(done, 16)

            load(h_in, 0, h_loaded)
            sp.dma_start(alibi, alibi_c).then_inc(alibi_in, 16)

            def step(i, on):
                if isinstance(i, int) and i == 0:
                    sp.wait_ge(wo_lo, WO_PARTS // 2)
                    sp.dma_start(stage[:, 0:ZT * HID].rearrange("p (m k) -> p m k", m=KT),
                                 bw.rearrange("(m p) k -> p m k", p=P)).then_inc(b_in, 16)
                if on("next"):
                    if not isinstance(i, int) or i + 2 < TILES:
                        filled(sp, "x1_1", i)
                        load(h_in, i + 2, h_loaded)
                if on("ffn"):
                    emptied(sp, "f_0", i)
                    apart(sp)
                    emptied(sp, "f_1", i)
                    sp.dma_start(out[bass.ds((i - 2) * P, P), :], h_out).then_inc(out_stored, 16)
                if on("attn"):
                    if on("proj"):
                        emptied(sp, "o_0", i)
                        apart(sp)
                        emptied(sp, "o_1", i)
                    load(h_res, i, hres_loaded)

            steps(sp, step)
            sp.wait_ge(out_stored, 16 * TILES)

        @block.tensor
        def _(pe):
            eye = ident[:, :]
            pe.wait_ge(const_in, 16 * 5)
            for src, at in ((al_s, 0), (ph_s, 1)):
                for half in range(2):
                    mm = pe.matmul(ps[half * 64:half * 64 + 64, at, 0:SEQ], src, ident[0:SEQ, 0:SEQ],
                                   start=True, stop=True)
            mm.then_inc(poles_T, 1)
            pe.matmul(ps[0:RDIM, 2, 0:NE], keys_s[0:NE, :], ident[0:NE, 0:NE],
                      start=True, stop=True).then_inc(keys_T, 1)
            pe.wait_ge(keys_Ts, 1)
            for k in range(KT):
                mm = pe.matmul(ps[:, 3, k * NE:(k + 1) * NE], wq_s[:, k * P:(k + 1) * P], keysT_s[:, :],
                               start=True, stop=True)
            mm.then_inc(router_filled, 1)
            pe.wait_ge(poles_copied, 2)

            def chunk_turn(n, j, b):
                pe.wait_ge(x_in[b], 16 * (j + 1))
                wait(pe, d_parts_ready, n - 1)
                apart(pe)
                v = xin[b].rearrange("c (h n t) -> c h t n", h=HC, t=2)
                for t in range(2):
                    for h in range(HC):
                        for half in range(2):
                            mm = pe.matmul(ps[half * 64:half * 64 + 64, b, (t * HC + h) * 64:(t * HC + h + 1) * 64],
                                           v[:, h, t, :], ident[0:BATCH, 0:BATCH], start=True, stop=True)
                mm.then_inc(xT_ready, 1)

            def chunk_contract(n, b):
                wait(pe, r_ready, n + 1)
                wait(pe, d_ready, n + 1)
                for h in range(HC):
                    wait(pe, krow_ready, HC * (n - 1) + h + 1)
                    for q in range(2):
                        mm = pe.matmul(ps[:, 4 + h, q * RW_:(q + 1) * RW_],
                                       d_full[b][:, h * DW_ + q * P:h * DW_ + (q + 1) * P],
                                       r_full[b][:, h * RW_:(h + 1) * RW_], start=True, stop=True)
                    mm.then_inc(k_ready, 1)

            for b in range(2):
                chunk_turn(b, 0, b)
            chunk_contract(0, 0)
            chunk_turn(2, 1, 0)
            chunk_contract(1, 1)
            chunk_turn(3, 1, 1)
            with pe.Fori(1, CHUNKS // 2 - 1) as j:
                for b in range(2):
                    chunk_contract(2 * j + b, b)
                    chunk_turn(2 * j + b + 2, j + 1, b)
            for b in range(2):
                chunk_contract(CHUNKS - 2 + b, b)
            pe.wait_ge(krow_ready, SEQ)

            def prepare(n):
                w, g, part = PREPS[n]
                src, _ = ffn_weight(w)
                if n in (0, KT):
                    pe.wait_ge(wscale, w + 1)
                if KT <= n < KT + 4:
                    take_bank(pe, f"s_{n % 4}", 1)
                wait(pe, prep_free, n - 3)
                for m in range(4):
                    mm = pe.transpose(bank[f"sc{n % 4}"][:, m * P:(m + 1) * P],
                                      src[:, 4 * part + m, g * P:(g + 1) * P], eye)
                mm.then_inc(prep_full, 1)

            for n in range(KT):
                prepare(n)
            pe.wait_ge(prep_free, KT)

            PASSES = ((0, 0), (0, 1), (1, 0))

            def product(dst, xt, w, ktiles, cols):
                return product_part(dst, xt, w, ktiles, cols, 0, ktiles)

            def product_part(dst, xt, w, ktiles, cols, k0, k1):
                for k in range(k0, k1):
                    for n, (s, ws) in enumerate(PASSES):
                        mm = pe.matmul(dst, xt[:, s, k, :], w[:, ws, k, cols],
                                       start=(k == 0 and n == 0), stop=(k == ktiles - 1 and n == 2))
                return mm

            def fill(user, i, mm):
                mm.then_inc(full[BANK_OF[user]], 1)

            def turn(user, i, src, k0, nk):
                take_bank(pe, user, i)
                for k in range(nk):
                    mm = pe.transpose(bank[BANK_OF[user]][:, k * P:(k + 1) * P],
                                      src[:, (k0 + k) * P:(k0 + k + 1) * P], eye)
                fill(user, i, mm)

            def step(i, on):
                if isinstance(i, int) and i == 0:
                    pe.wait_ge(wqkv_lo, KT)
                    pe.wait_ge(router_lo, 1)
                    pe.wait_ge(blocks_zero, 1)
                preparing = isinstance(i, int) and i == 1
                if on("attn"):
                    emptied(pe, "x1_1", i - 1)
                    take_bank(pe, "kv", i)
                    fill("kv", i, product(bank["small"][:, 0:2 * DH], x1T, wqkv_s, KT, slice(HID, QKV)))
                if on("attn"):
                    take_bank(pe, "q_0", i)
                    for k in range(KT):
                        mm = product_part(bank["wide0"], x1T, wqkv_s, KT, slice(0, HALF), k, k + 1)
                        if k == KT - 1:
                            fill("q_0", i, mm)
                        if preparing and k % 2:
                            prepare(KT + k // 2)
                    wait(pe, keys_copied, i + 1)
                    turn("kT", i, k_rep, 0, 1)
                if on("ffn"):
                    wait(pe, xn2_ready, i - 1)
                    turn("x2_0", i, xn2, 0, 4)
                if on("attn"):
                    take_bank(pe, "q_1", i)
                    product_part(bank["wide1"], x1T, wqkv_s, KT, slice(HALF, HID), 0, 4)
                    if preparing:
                        for n in (4, 5):
                            prepare(KT + n)
                if on("ffn"):
                    turn("x2_1", i, xn2, 4, 4)
                if on("attn"):
                    fill("q_1", i, product_part(bank["wide1"], x1T, wqkv_s, KT, slice(HALF, HID), 4, KT))
                if preparing:
                    for n in (6, 7):
                        prepare(KT + n)
                    pe.wait_ge(prep_free, len(PREPS))
                if on("ffn"):
                    emptied(pe, "x2_1", i)
                    take_bank(pe, "r", i)
                    fill("r", i, product(bank["small"][:, 0:NE], x2T, wr_s, KT, slice(0, NE)))
                    take_bank(pe, "z", i)
                    product_part(bank["wide0"], x2T, wa_s, KT, slice(0, BOT), 0, 2)
                if on("attn"):
                    emptied(pe, "q_0", i)
                    turn("qT_0", i, q_row, 0, 4)
                if on("ffn"):
                    product_part(bank["wide0"], x2T, wa_s, KT, slice(0, BOT), 2, 6)
                if on("attn"):
                    emptied(pe, "q_1", i)
                    turn("qT_1", i, q_row, 4, 4)
                if on("ffn"):
                    fill("z", i, product_part(bank["wide0"], x2T, wa_s, KT, slice(0, BOT), 6, KT))

                def scores(n):
                    take_bank(pe, f"s_{n}", i)
                    emptied(pe, f"qT_{n // 2}", i)
                    if n == 0:
                        emptied(pe, "kT", i)
                    for g in range(2):
                        for b in range(2):
                            for m, (s, ks) in enumerate(PASSES):
                                mm = pe.matmul(bank[f"sc{n}"][b * 64:(b + 1) * 64, g * 256:(g + 1) * 256],
                                               qT[:, s, 2 * n + g, b * 64:(b + 1) * 64],
                                               k_blk[:, ks, b, :, :].rearrange("p j k -> p (j k)"),
                                               start=(m == 0), stop=(m == 2))
                    fill(f"s_{n}", i, mm)

                if on("attn"):
                    scores(0)
                    scores(1)
                if on("ffn"):
                    emptied(pe, "z", i)
                    turn("zT", i, zg, 0, ZT)
                if on("attn"):
                    scores(2)
                    scores(3)
                if on("ffn"):
                    emptied(pe, "zT", i)
                    take_bank(pe, "f_0", i)
                    product_part(bank["wide1"], zT, wb_s, ZT, slice(0, HALF), 0, 2)
                if on("next"):
                    wait(pe, xn1_ready, i + 2)
                    turn("x1_0", i, xn1, 0, 4)
                if on("ffn"):
                    fill("f_0", i, product_part(bank["wide1"], zT, wb_s, ZT, slice(0, HALF), 2, ZT))
                    take_bank(pe, "f_1", i)
                    product_part(bank["wide0"], zT, wb_s, ZT, slice(HALF, HID), 0, 2)
                if on("next"):
                    turn("x1_1", i, xn1, 4, 4)
                if on("ffn"):
                    fill("f_1", i, product_part(bank["wide0"], zT, wb_s, ZT, slice(HALF, HID), 2, ZT))
                if on("proj"):
                    if isinstance(i, int) and i == 1:
                        pe.wait_ge(wo_lo, WO_PARTS)
                    emptied(pe, "a_1", i - 1)
                    take_bank(pe, "o_0", i)
                    fill("o_0", i, product(bank["wide1"], attT, wo_s, KT, slice(0, HALF)))
                    take_bank(pe, "o_1", i)
                    fill("o_1", i, product(bank["wide0"], attT, wo_s, KT, slice(HALF, HID)))
                if on("attn"):
                    for u in range(4):
                        wait(pe, probs_ready, 4 * i + u + 1)
                        take_bank(pe, f"p_{u}", i)
                        for m in range(4):
                            mm = pe.transpose(bank[f"sc{u}"][:, m * P:(m + 1) * P],
                                              probs[:, (4 * u + m) * P:(4 * u + m + 1) * P], eye)
                        fill(f"p_{u}", i, mm)
                    for u in range(4):
                        emptied(pe, f"p_{u}", i)
                        if u == 0:
                            emptied(pe, "kv", i)
                        att = bank[f"sc{u // 2}"].rearrange("p (c b t) -> p c b t", c=4, b=2)
                        for b in range(2):
                            for m in range(2):
                                mm = pe.matmul(att[m * 64:(m + 1) * 64, 2 * (u % 2):2 * (u % 2) + 2, b, :],
                                               v_blk[:, b, :], pT[:, 4 * u + m:4 * u + 4:2, b * 64:(b + 1) * 64],
                                               start=True, stop=True)
                        if u % 2 == 1:
                            fill(f"a_{u // 2}", i, mm)

            steps(pe, step)

        @block.scalar
        def _(act):
            cp = ACT.Copy
            act.wait_ge(keys_T, 1)
            act.activation(keysT_s[:, :], ps[0:RDIM, 2, 0:NE], cp).then_inc(keys_Ts, 1)
            act.wait_ge(exponent_ready, 1)
            act.activation(etab, etab, ACT.Exp).then_inc(exp_done, 1)
            re, im, every = slice(0, MODES), slice(MODES, P), slice(0, P)
            act.wait_ge(quarter_set, 2)
            act.wait_ge(turn_ready, 1)
            for v, rows, cols, sign in ((0, im, A_COLS, -1), (0, im, Q_COLS, 1),
                                        (1, re, slice(0, NA + NQ), -1), (1, every, B_COLS, 1)):
                act.activation(vtab[v][rows, :, cols], turn[rows, :, cols], ACT.Sin,
                               scale=sign * TURN).then_inc(sin_done, 1)
            act.wait_ge(turn_ready, 2)
            for v, rows, cols, sign in ((0, re, slice(0, NA + NQ), 1), (0, every, B_COLS, 1),
                                        (1, im, A_COLS, -1), (1, im, Q_COLS, 1)):
                bias = quarter[rows, 0:1] if sign == 1 else quarter[rows, 1:2]
                act.activation(vtab[v][rows, :, cols], turn_abs[rows, :, cols], ACT.Sin, bias=bias,
                               scale=-sign * TURN).then_inc(sin_done, 1)
            act.wait_ge(wscale, RW + 1)
            act.activation(wr_s[:, 0, :, :].rearrange("p k e -> p (k e)"), ps[:, 3, :], cp,
                           scale=scales[:, RW, 4:5]).then_inc(router_hi, 1)
            def chunk(n, j, b):
                if not isinstance(j, int) or j > 0:
                    act.wait_ge(k_stored[b], 64 * j)
                for h in range(HC):
                    wait(act, k_ready, HC * n + h + 1)
                    act.activation(krow[b][:, h * HALF:(h + 1) * HALF], ps[:, 4 + h, :], cp).then_inc(krow_ready, 1)

            for b in range(2):
                chunk(b, 0, b)
            for b in range(2):
                chunk(2 + b, 1, b)
                if b == 0:
                    act.wait_ge(wscale, QW + 1)
                for k in range(b * KT // 2, (b + 1) * KT // 2):
                    act.activation(wqkv_s[:, 0, k, :], stage[:, k * QKV:(k + 1) * QKV], cp,
                                   scale=scales[:, QW, 4:5]).then_inc(wqkv_hi, 1)
            with act.Fori(2, CHUNKS // 2) as j:
                for b in range(2):
                    chunk(2 * j + b, j, b)

            def prepare(n):
                w, g, part = PREPS[n]
                act.wait_ge(prep_full, n + 1)
                act.activation(ffn_weight(w)[1][:, 0, g, part * HALF:(part + 1) * HALF], bank[f"sc{n % 4}"], cp,
                               scale=scales[:, w, 4:5]).then_inc(prep_hi, 1)

            def split_wo(m):
                n = KT // WO_PARTS
                act.activation(wo_s[:, 0, m * n:(m + 1) * n, :],
                               stage[:, m * n * HID:(m + 1) * n * HID].rearrange("p (k n) -> p k n", n=HID), cp,
                               scale=scales[:, OW, 4:5]).then_inc(wo_hi, 1)

            act.wait_ge(wscale, AW + 1)
            for n in range(KT):
                prepare(n)
            phase1_over(act)

            def hi(user, i, dst):
                filled(act, user, i)
                act.activation(dst, bank[BANK_OF[user]], cp).then_inc(hi_done, 1)

            def evac(user, i, dst):
                filled(act, user, i)
                act.activation(dst, bank[BANK_OF[user]], cp).then_inc(free[BANK_OF[user]], 1)

            def halves(t, k0, nk):
                return t[:, 0, k0:k0 + nk, :].rearrange("p k t -> p (k t)")

            def step(i, on):
                preparing = isinstance(i, int) and i == 1
                if on("attn"):
                    filled(act, "kv", i)
                    act.activation(k_rep.rearrange("p (j d) -> p j d", j=4),
                                   bank["small"][:, 0:DH].unsqueeze(1).broadcast_to([P, 4, DH]),
                                   cp).then_inc(keys_copied, 1)
                    for b in range(2):
                        for m in range(2):
                            ins = act.activation(v_blk[m * 64:(m + 1) * 64, b, m * DH:(m + 1) * DH],
                                                 bank["small"][b * 64:(b + 1) * 64, DH:2 * DH], cp)
                    ins.then_inc(free["small"], 1)
                    if preparing:
                        for n in range(4):
                            prepare(KT + n)
                    if isinstance(i, int) and i == 0:
                        act.wait_ge(wscale, OW + 1)
                        split_wo(0)
                    evac("q_0", i, q_row[:, 0:HALF])
                    filled(act, "kT", i)
                    for j in range(4):
                        rows = slice(j * 32, j * 32 + 32)
                        ins = act.activation(k_blk[rows, 0, :, j, :],
                                             bank["small"][rows, 0:P].rearrange("p (b k) -> p b k", b=2), cp)
                    ins.then_inc(keys_hi, 1)
                    if isinstance(i, int) and i == 0:
                        split_wo(1)
                if on("ffn"):
                    hi("x2_0", i, halves(x2T, 0, 4))
                    hi("x2_1", i, halves(x2T, 4, 4))
                if on("attn"):
                    if preparing:
                        for n in range(4, 8):
                            prepare(KT + n)
                    evac("q_1", i, q_row[:, HALF:HID])
                    hi("qT_0", i, halves(qT, 0, 4))
                if on("ffn"):
                    wait(act, route, 8 * (i - 2) + 6)
                    act.activation(r_exp, r_exp, ACT.Exp).then_inc(route_exp, 1)
                if on("attn"):
                    hi("qT_1", i, halves(qT, 4, 4))
                    if isinstance(i, int) and i == 0:
                        split_wo(2)
                if on("ffn"):
                    filled(act, "zT", i)
                    act.activation(halves(zT, 0, ZT), bank["turn"], cp).then_inc(hi_done, 1)
                if on("next"):
                    hi("x1_0", i, halves(x1T, 0, 4))
                    hi("x1_1", i, halves(x1T, 4, 4))
                if on("attn"):
                    for n in range(2):
                        wait(act, shifted, 2 * i + n + 1)
                        v = probs[:, n * 1024:(n + 1) * 1024]
                        act.activation(v, v, ACT.Exp).then_inc(exps_done, 1)
                    if isinstance(i, int) and i == 0:
                        split_wo(3)
                    for u in range(4):
                        evac(f"p_{u}", i, pT[:, 4 * u:4 * u + 4, :].rearrange("p u t -> p (u t)"))
                    for u in range(2):
                        hi(f"a_{u}", i, halves(attT, 4 * u, 4))

            steps(act, step)

        @block.gpsimd
        def _(pool):
            def link(ins, n):
                ins.then_inc(pool_steps, 1)
                pool.wait_ge(pool_steps, n)

            pool.memset(quarter[:, 0:1], math.pi / 2).then_inc(quarter_set, 1)
            pool.memset(quarter[:, 1:2], -math.pi / 2).then_inc(quarter_set, 1)
            pool.wait_ge(poles_copied, 2)
            pool.wait_ge(tab_in, 16)
            pool.tensor_tensor(etab, aT.unsqueeze(2).broadcast_to([P, SEQ, TK]),
                               times[:, 0, :].unsqueeze(1).broadcast_to([P, SEQ, TK]),
                               ALU.mult).then_inc(exponent_ready, 1)

            def scale_of_all(w):
                pool.wait_ge(wmax, w + 1)
                pool.partition_all_reduce(scales[:, w, 1:2], scales[:, w, 0:1], P, RMAX).then_inc(wmax_all, 1)

            re, im, t2, t0, t1, t3, t4, gre, gim = (g4[:, k, :] for k in range(9))
            one = NA + NQ + 1
            pool.wait_ge(exp_done, 1)
            pool.wait_ge(sin_done, 8)
            pool.tensor_tensor(re, vtab[0][:, :, one], etab[:, :, one], ALU.mult).then_inc(pole_read, 1)
            pool.tensor_tensor(im, vtab[1][:, :, one], etab[:, :, one], ALU.mult).then_inc(pole_read, 1)
            pool.wait_ge(pole_read, 2)
            link(pool.tensor_scalar(re, re, -1.0, None, ALU.add), 1)
            scale_of_all(RW)
            pool.tensor_tensor(t0, re, aT, ALU.mult)
            pool.tensor_tensor(t1, im, phT, ALU.mult)
            pool.tensor_tensor(t3, im, aT, ALU.mult)
            link(pool.tensor_tensor(t4, re, phT, ALU.mult), 2)
            pool.tensor_tensor(gre, t0, t1, ALU.add)
            link(pool.tensor_tensor(gim, t3, t4, ALU.subtract), 3)
            pool.wait_ge(poles_inverse, 1)
            pool.tensor_tensor(gre, gre, t2, ALU.mult).then_inc(g_ready, 1)
            pool.tensor_tensor(gim, gim, t2, ALU.mult).then_inc(g_ready, 1)

            def chunk(n, b):
                wait(pool, r_parts_ready, n + 1)
                pool.tensor_tensor(r_full[b], r_full[b], r_term, ALU.add).then_inc(r_ready, 1)
                wait(pool, d_parts_ready, n + 1)
                pool.tensor_tensor(d_full[b], d_full[b], d_term, ALU.add).then_inc(d_ready, 1)

            for b in range(2):
                chunk(b, b)
            scale_of_all(QW)
            with pool.Fori(1, CHUNKS // 2) as j:
                for b in range(2):
                    chunk(2 * j + b, b)
            scale_of_all(AW)
            phase1_over(pool)
            link(pool.memset(k_blk, 0.0), 4)
            link(pool.memset(v_blk, 0.0), 5)
            pool.memset(half_neg, -0.5).then_inc(blocks_zero, 1)
            pool.wait_ge(blocks_zero, 1)

            def rstd(l, n):
                done, v, base = rsd[l], rs[:, l, :], 6 * (n)
                wait(pool, mv_ready[l], n + 1)
                apart(pool)
                pool.tensor_scalar(v[:, 0:1], mv[:, l, 1:2], EPS, None, ALU.add).then_inc(done, 1)
                pool.wait_ge(done, base + 1)
                pool.tensor_tensor(v[:, 1:2], v[:, 0:1], half_neg, ALU.pow).then_inc(done, 1)
                pool.wait_ge(done, base + 2)
                pool.tensor_tensor(v[:, 2:3], v[:, 1:2], v[:, 1:2], ALU.mult).then_inc(done, 1)
                pool.wait_ge(done, base + 3)
                pool.tensor_tensor(v[:, 3:4], v[:, 2:3], v[:, 0:1], ALU.mult).then_inc(done, 1)
                pool.wait_ge(done, base + 4)
                apart(pool)
                pool.tensor_scalar(v[:, 4:5], v[:, 3:4], -0.5, 1.5, ALU.mult, ALU.add).then_inc(done, 1)
                pool.wait_ge(done, base + 5)
                pool.tensor_tensor(v[:, 5:6], v[:, 1:2], v[:, 4:5], ALU.mult).then_inc(done, 1)

            def step(i, on):
                if on("next"):
                    rstd(0, i + 1)
                if isinstance(i, int) and i == -1:
                    scale_of_all(OW)
                if on("proj"):
                    rstd(1, i - 1)
                if isinstance(i, int) and i == 0:
                    scale_of_all(BW)

            steps(pool, step)

        @block.vector
        def _(dve):
            cnt = [0]

            def link(ins):
                cnt[0] += 1
                ins.then_inc(dve_steps, 1)
                dve.wait_ge(dve_steps, cnt[0])

            def wrap(dst, src, n_):
                link(dve.tensor_scalar(n_, src, 1 / (2 * math.pi), ROUND, ALU.mult, ALU.add))
                link(dve.tensor_scalar(n_, n_, ROUND, None, ALU.subtract))
                link(dve.scalar_tensor_tensor(dst, n_, -TWO_PI_HI, src, ALU.mult, ALU.add))
                link(dve.scalar_tensor_tensor(dst, n_, -TWO_PI_LO, dst, ALU.mult, ALU.add))

            dve.wait_ge(poles_T, 1)
            dve.tensor_copy(aT, ps[:, 0, 0:SEQ]).then_inc(poles_copied, 1)
            dve.tensor_copy(phT, ps[:, 1, 0:SEQ]).then_inc(poles_copied, 1)
            dve.wait_ge(poles_copied, 2)
            wrap(phT, phT, g4[:, 3, :])
            p_hi, p_lo, p_sum, p_tmp = (g4[:, k, :] for k in range(4))
            link(dve.tensor_scalar(p_hi, phT, 1 / (2 * math.pi), ROUND_13, ALU.mult, ALU.add))
            link(dve.tensor_scalar(p_hi, p_hi, ROUND_13, None, ALU.subtract))
            for m, power in ((0, NB), (1, NA * NB)):
                link(dve.tensor_scalar(units[:, m, :], p_hi, float(power), None, ALU.mult))
            link(dve.scalar_tensor_tensor(p_lo, p_hi, -TWO_PI_HI, phT, ALU.mult, ALU.add))
            link(dve.scalar_tensor_tensor(p_lo, p_hi, -TWO_PI_LO, p_lo, ALU.mult, ALU.add))
            link(dve.tensor_scalar(p_lo, p_lo, 1 / (2 * math.pi), None, ALU.mult))
            link(dve.tensor_tensor(p_sum, p_hi, p_lo, ALU.add))
            whole = g4[:, 4:6, :]
            link(dve.tensor_scalar(whole, units, ROUND, ROUND, ALU.add, ALU.subtract))
            link(dve.tensor_tensor(units, units, whole, ALU.subtract))
            for m, power in ((0, NB), (1, NA * NB)):
                link(dve.scalar_tensor_tensor(units[:, m, :], p_lo, float(power), units[:, m, :], ALU.mult, ALU.add))
            dve.wait_ge(tab_in, 16)
            for unit, cols in ((units[:, 0, :], A_COLS), (units[:, 1, :], Q_COLS), (p_sum, B_COLS)):
                w = cols.stop - cols.start
                ins = dve.tensor_tensor(turn[:, :, cols], unit.unsqueeze(2).broadcast_to([P, SEQ, w]),
                                        times[:, 1, cols].unsqueeze(1).broadcast_to([P, SEQ, w]), ALU.mult)
                link(ins)
            link(dve.tensor_scalar(turn_abs, turn, ROUND, ROUND, ALU.add, ALU.subtract))
            dve.tensor_tensor(turn, turn, turn_abs, ALU.subtract).then_inc(turn_ready, 1)
            dve.wait_ge(turn_ready, 1)
            dve.tensor_scalar(turn_abs.bitcast(I32), turn.bitcast(I32), 0x7FFFFFFF, None,
                              ALU.bitwise_and).then_inc(turn_ready, 1)

            def weight_max(w, view):
                dve.tensor_reduce(scales[:, w, 0:1], view, AX, ALU.max, apply_absolute_value=True).then_inc(wmax, 1)

            def weight_scale(w):
                dve.wait_ge(wmax_all, w + 1)
                link(dve.tensor_scalar(scales[:, w, 1:2], scales[:, w, 1:2], 1e-30, None, ALU.max))
                link(dve.tensor_scalar(scales[:, w, 2:3].bitcast(I32), scales[:, w, 1:2].bitcast(I32),
                                       0x7F800000, None, ALU.bitwise_and))
                link(dve.reciprocal(scales[:, w, 3:4], scales[:, w, 2:3]))
                link(dve.tensor_scalar(scales[:, w, 5:6], scales[:, w, 2:3], 0.125, None, ALU.mult))
                dve.tensor_scalar(scales[:, w, 4:5], scales[:, w, 3:4], 8.0, None, ALU.mult).then_inc(wscale, 1)
                dve.wait_ge(wscale, w + 1)

            dve.wait_ge(wqkv_in, 16)
            wqkv_cut = KT // 2 * QKV
            dve.tensor_reduce(scales[:, QW, 1:2], stage[:, 0:wqkv_cut], AX, ALU.max, apply_absolute_value=True)
            dve.wait_ge(router_filled, 1)
            weight_max(RW, ps[:, 3, :])
            den, t0 = g4[:, 2, :], units[:, 0, :]
            link(dve.scalar_tensor_tensor(den, aT, 0.5, aT, ALU.mult, ALU.mult))
            link(dve.scalar_tensor_tensor(t0, phT, 0.5, phT, ALU.mult, ALU.mult))
            link(dve.tensor_tensor(t0, den, t0, ALU.add))
            dve.reciprocal(den, t0).then_inc(poles_inverse, 1)
            dve.wait_ge(pole_read, 2)
            link(dve.tensor_tensor(vtab[0], vtab[0], etab, ALU.mult))
            weight_scale(RW)
            link(dve.tensor_tensor(vtab[1], vtab[1], etab, ALU.mult))
            dve.wait_ge(g_ready, 2)
            s1, s2 = (vtab[v][:, :, Q_COLS] for v in range(2))
            grb, gib = (g4[:, k, :].unsqueeze(2).broadcast_to([P, SEQ, NQ]) for k in (7, 8))
            tmp = [turn[:, :, v * NQ:(v + 1) * NQ] for v in range(2)]
            dve.tensor_tensor(gtab[0], s1, grb, ALU.mult)
            dve.tensor_tensor(tmp[0], s2, gib, ALU.mult)
            dve.tensor_tensor(gtab[1], s2, grb, ALU.mult)
            link(dve.tensor_tensor(tmp[1], s1, gib, ALU.mult))
            dve.tensor_tensor(gtab[0], gtab[0], tmp[0], ALU.add).then_inc(tabs_ready, 1)
            dve.tensor_tensor(gtab[1], gtab[1], tmp[1], ALU.subtract).then_inc(tabs_ready, 1)
            dve.wait_ge(tabs_ready, 2)

            dve.wait_ge(router_hi, 1)
            dve.scalar_tensor_tensor(wr_s[:, 1, :, :].rearrange("p k e -> p (k e)"), ps[:, 3, :], scales[:, RW, 4:5],
                                     wr_s[:, 0, :, :].rearrange("p k e -> p (k e)"),
                                     ALU.mult, ALU.subtract).then_inc(router_lo, 1)

            def chunk(n, b):
                hs = bass.ds(n * HC, HC)

                def r_product(dst, v):
                    alpha = vtab[v][:, hs, A_COLS].unsqueeze(3).broadcast_to([P, HC, NA, NB])
                    beta = vtab[v][:, hs, B_COLS].unsqueeze(2).broadcast_to([P, HC, NA, NB])
                    return dve.tensor_tensor(dst.rearrange("p (h a b) -> p h a b", h=HC, a=NA), alpha, beta, ALU.mult)

                def d_product(dst, v):
                    xs = ps[:, b, v * HC * 64:(v + 1) * HC * 64].rearrange("p (h c) -> p h c", h=HC)
                    return dve.tensor_tensor(dst.rearrange("p (h q c) -> p h q c", h=HC, q=NQ),
                                             xs.unsqueeze(2).broadcast_to([P, HC, NQ, BATCH]),
                                             gtab[v][:, hs, :].unsqueeze(3).broadcast_to([P, HC, NQ, BATCH]), ALU.mult)

                wait(dve, r_ready, n)
                r_product(r_term, 1)
                wait(dve, k_ready, HC * (n - 1))
                r_product(r_full[b], 0).then_inc(r_parts_ready, 1)
                wait(dve, xT_ready, n + 1)
                d_product(d_full[b], 0)
                wait(dve, d_ready, n)
                d_product(d_term, 1).then_inc(d_parts_ready, 1)

            for b in range(2):
                chunk(b, b)
            link(dve.tensor_reduce(scales[:, QW, 2:3], stage[:, wqkv_cut:KT * QKV], AX, ALU.max,
                                   apply_absolute_value=True))
            dve.tensor_tensor(scales[:, QW, 0:1], scales[:, QW, 1:2], scales[:, QW, 2:3], ALU.max).then_inc(wmax, 1)
            chunk(2, 0)
            weight_scale(QW)
            chunk(3, 1)
            with dve.Fori(2, 2 + KT // 2) as j:
                for b in range(2):
                    chunk(2 * j + b, b)
                    wait(dve, wqkv_hi, 2 * j + b - 3)
                    k = bass.ds(2 * j + b - 4, 1)
                    dve.scalar_tensor_tensor(
                        wqkv_s[:, 1, k, :], stage[:, :].rearrange("p (k n) -> p k n", k=KT)[:, k, :],
                        scales[:, QW, 4:5], wqkv_s[:, 0, k, :], ALU.mult, ALU.subtract).then_inc(wqkv_lo, 1)
            with dve.Fori(2 + KT // 2, CHUNKS // 2) as j:
                for b in range(2):
                    chunk(2 * j + b, b)
            dve.wait_ge(a_in, 16)
            weight_max(AW, stage_a)
            dve.wait_ge(wo_in, 16 * KT)
            wo_cut = KT // 4 * HID
            dve.tensor_reduce(scales[:, OW, 1:2], stage[:, 0:wo_cut], AX, ALU.max, apply_absolute_value=True)
            weight_scale(AW)
            inv = [scales[:, w, 5:6] for w in range(5)]
            c_score, c_proj, c_ffn = (consts[:, k:k + 1] for k in range(3))

            def prepare(n):
                w, g, part = PREPS[n]
                cols, dst = slice(part * HALF, (part + 1) * HALF), ffn_weight(w)[1]
                dve.wait_ge(prep_hi, n + 1)
                dve.scalar_tensor_tensor(dst[:, 1, g, cols], bank[f"sc{n % 4}"], scales[:, w, 4:5],
                                         dst[:, 0, g, cols], ALU.mult, ALU.subtract).then_inc(prep_free, 1)

            for n in range(KT):
                prepare(n)
            link(dve.scalar_tensor_tensor(c_score, inv[QW], SOFT_SCALE, inv[QW], ALU.mult, ALU.mult))
            phase1_over(dve)

            def lo(user, i, t, k0, nk):
                wait(dve, hi_done, hi_after(user, i))
                dve.tensor_tensor(t[:, 1, k0:k0 + nk, :].rearrange("p k t -> p (k t)"), bank[BANK_OF[user]],
                                  t[:, 0, k0:k0 + nk, :].rearrange("p k t -> p (k t)"),
                                  ALU.subtract).then_inc(free[BANK_OF[user]], 1)

            def norm_stats(l, src, n):
                for k in range(2):
                    dve.bn_stats(bn[:, l, 6 * k:6 * k + 6], src[:, k * HALF:(k + 1) * HALF]).then_inc(stats1, 1)
                wait(dve, stats1, 2 * (n + 1))
                apart(dve)
                dve.bn_aggr(mv[:, l, :], bn[:, l, :]).then_inc(mv_ready[l], 1)

            def normalise(l, src, dst, n, done):
                wait(dve, rsd[l], 6 * (n + 1))
                dve.tensor_scalar(dst, src, mv[:, l, 0:1], rs[:, l, 5:6], ALU.subtract, ALU.mult).then_inc(done, 1)

            def split_wo(m):
                n = KT // WO_PARTS
                cols = slice(m * n * HID, (m + 1) * n * HID)
                dve.wait_ge(wo_hi, m + 1)
                dve.scalar_tensor_tensor(wo_s[:, 1, m * n:(m + 1) * n, :].rearrange("p k n -> p (k n)"),
                                         stage[:, cols], scales[:, OW, 4:5],
                                         wo_s[:, 0, m * n:(m + 1) * n, :].rearrange("p k n -> p (k n)"),
                                         ALU.mult, ALU.subtract).then_inc(wo_lo, 1)

            def step(i, on):
                if on("next"):
                    wait(dve, h_loaded, 16 * (i + 2))
                    norm_stats(0, h_in, i + 1)
                if on("attn"):
                    wait(dve, keys_hi, i + 1)
                    for j in range(4):
                        rows = slice(j * 32, j * 32 + 32)
                        ins = dve.tensor_tensor(k_blk[rows, 1, :, j, :],
                                                bank["small"][rows, 0:P].rearrange("p (b k) -> p b k", b=2),
                                                k_blk[rows, 0, :, j, :], ALU.subtract)
                    ins.then_inc(free["small"], 1)
                if on("ffn"):
                    lo("x2_0", i, x2T, 0, 4)
                    lo("x2_1", i, x2T, 4, 4)
                if on("next"):
                    normalise(0, h_in, xn1, i + 1, xn1_ready)
                if isinstance(i, int) and i == 0:
                    split_wo(0)
                if isinstance(i, int) and i == 1:
                    for n in range(KT, len(PREPS)):
                        prepare(n)
                if on("ffn"):
                    t = i - 2
                    filled(dve, "r", i)
                    base = 8 * t
                    dve.tensor_scalar(r_sc, bank["small"][:, 0:NE], inv[RW], None, ALU.mult).then_inc(free["small"], 1)
                    emptied(dve, "r", i)
                    apart(dve)
                    dve.max(m8a, r_sc).then_inc(route, 1)
                    wait(dve, route, base + 1)
                    apart(dve)
                    dve.match_replace(r_w1, m8a, r_sc, TAKEN).then_inc(route, 1)
                    wait(dve, route, base + 2)
                    apart(dve)
                    dve.max(m8b, r_w1).then_inc(route, 1)
                    wait(dve, route, base + 3)
                    apart(dve)
                    dve.match_replace(r_w2, m8b, r_w1, TAKEN).then_inc(route, 1)
                    wait(dve, route, base + 4)
                    dve.tensor_scalar(r_sel, r_w2, TAKEN, None, ALU.is_equal).then_inc(route, 1)
                    dve.tensor_scalar(r_exp, r_sc, m8a[:, 0:1], None, ALU.subtract).then_inc(route, 1)
                    wait(dve, route_exp, t + 1)
                    dve.scalar_tensor_tensor(r_gate, r_exp, 1.0, r_sel, ALU.mult, ALU.mult,
                                             accum_out=r_one[:, 0:1]).then_inc(route, 1)
                    wait(dve, route, base + 7)
                    dve.reciprocal(r_one[:, 1:2], r_one[:, 0:1]).then_inc(route, 1)
                if on("attn"):
                    lo("qT_0", i, qT, 0, 4)
                    if isinstance(i, int) and i == 0:
                        split_wo(1)
                    lo("qT_1", i, qT, 4, 4)
                if on("ffn"):
                    wait(dve, route, base + 8)
                    filled(dve, "z", i)
                    dve.scalar_tensor_tensor(zg.rearrange("p (e r) -> p e r", r=RANK),
                                             bank["wide0"].rearrange("p (e r) -> p e r", r=RANK), r_one[:, 1:2],
                                             r_gate.unsqueeze(2).broadcast_to([P, NE, RANK]),
                                             ALU.mult, ALU.mult).then_inc(free["wide0"], 1)

                def biased(n):
                    filled(dve, f"s_{n}", i)
                    cols = slice(n * HALF, (n + 1) * HALF)
                    dve.scalar_tensor_tensor(probs[:, cols], bank[f"sc{n}"], c_score, alibi[:, cols],
                                             ALU.mult, ALU.add).then_inc(free[f"sc{n}"], 1)

                p3 = probs.rearrange("p (h k) -> p h k", h=HEADS)

                def row_max(n):
                    emptied(dve, f"s_{2 * n + 1}", i)
                    hh = slice(n * 16, (n + 1) * 16)
                    dve.tensor_reduce(smax[:, hh], p3[:, hh, :], AX, ALU.max).then_inc(max_ready, 1)

                if on("attn"):
                    if isinstance(i, int) and i == 0:
                        dve.wait_ge(alibi_in, 16)
                    biased(0)
                    biased(1)
                if on("ffn"):
                    lo("zT", i, zT, 0, ZT)
                if on("attn"):
                    row_max(0)
                    biased(2)
                    biased(3)
                if on("attn"):
                    row_max(1)
                if on("next"):
                    lo("x1_0", i, x1T, 0, 4)

                def result(n, user):
                    filled(dve, user, i)
                    cols = slice(n * HALF, (n + 1) * HALF)
                    dve.scalar_tensor_tensor(h_out[:, cols], bank[BANK_OF[user]], c_ffn, h_mid[:, cols],
                                             ALU.mult, ALU.add).then_inc(free[BANK_OF[user]], 1)

                if on("ffn"):
                    wait(dve, out_stored, 16 * (i - 2))
                    result(0, "f_0")
                if on("attn"):
                    for n in range(2):
                        wait(dve, max_ready, 2 * i + n + 1)
                        hh = slice(n * 16, (n + 1) * 16)
                        dve.tensor_tensor(p3[:, hh, :], p3[:, hh, :],
                                          smax[:, hh].unsqueeze(2).broadcast_to([P, 16, SEQ]),
                                          ALU.subtract).then_inc(shifted, 1)
                if on("next"):
                    lo("x1_1", i, x1T, 4, 4)
                if on("ffn"):
                    result(1, "f_1")
                if on("attn"):
                    for n in range(2):
                        hh = slice(n * 16, (n + 1) * 16)
                        wait(dve, exps_done, 2 * i + n + 1)
                        dve.tensor_reduce(ssum[:, hh], p3[:, hh, :], AX, ALU.add).then_inc(sums, 1)
                        wait(dve, sums, 4 * i + 2 * n + 1)
                        dve.reciprocal(srec[:, hh], ssum[:, hh]).then_inc(sums, 1)
                        wait(dve, sums, 4 * i + 2 * n + 2)
                        for u in (2 * n, 2 * n + 1):
                            hh = slice(u * 8, (u + 1) * 8)
                            dve.tensor_tensor(p3[:, hh, :], p3[:, hh, :],
                                              srec[:, hh].unsqueeze(2).broadcast_to([P, 8, SEQ]),
                                              ALU.mult).then_inc(probs_ready, 1)
                if isinstance(i, int) and i == 0:
                    dve.wait_ge(b_in, 16)
                    weight_max(BW, stage[:, 0:ZT * HID])
                    weight_scale(BW)
                    link(dve.scalar_tensor_tensor(c_ffn, inv[AW], FFN_SCALE, inv[BW], ALU.mult, ALU.mult))
                if on("proj"):
                    wait(dve, hres_loaded, 16 * i)
                    for n, user in ((0, "o_0"), (1, "o_1")):
                        filled(dve, user, i)
                        cols = slice(n * HALF, (n + 1) * HALF)
                        dve.scalar_tensor_tensor(h_mid[:, cols], bank[BANK_OF[user]], c_proj, h_res[:, cols],
                                                 ALU.mult, ALU.add).then_inc(free[BANK_OF[user]], 1)
                        emptied(dve, user, i)
                        dve.bn_stats(bn[:, 1, 6 * n:6 * n + 6], h_mid[:, cols]).then_inc(stats2, 1)
                    wait(dve, stats2, 2 * i)
                    apart(dve)
                    dve.bn_aggr(mv[:, 1, :], bn[:, 1, :]).then_inc(mv_ready[1], 1)
                if on("attn"):
                    lo("a_0", i, attT, 0, 4)
                    lo("a_1", i, attT, 4, 4)
                if on("proj"):
                    normalise(1, h_mid, xn2, i - 1, xn2_ready)
                if isinstance(i, int) and i == -1:
                    link(dve.tensor_reduce(scales[:, OW, 2:3], stage[:, wo_cut:KT * HID], AX, ALU.max,
                                           apply_absolute_value=True))
                    dve.tensor_tensor(scales[:, OW, 0:1], scales[:, OW, 1:2], scales[:, OW, 2:3],
                                      ALU.max).then_inc(wmax, 1)
                    weight_scale(OW)
                    link(dve.tensor_tensor(c_proj, inv[QW], inv[OW], ALU.mult))
                if isinstance(i, int) and i == 0:
                    split_wo(2)
                    split_wo(3)

            steps(dve, step)


def _slopes(n):
    base = 2.0 ** (-2.0 ** (-(math.log2(n) - 3)))
    return (base ** np.arange(1, n + 1, dtype=np.float64)).astype(np.float32)


def _constants():
    ident = np.eye(P, dtype=np.float32)
    pos = np.arange(SEQ)
    bias = _slopes(HEADS)[None, :, None] * (pos[None, None, :] - pos[:, None, None]).astype(np.float32)
    bias = np.where(pos[None, None, :] <= pos[:, None, None], bias, np.float32(-1e30)).astype(np.float32)
    alibi = np.concatenate([bias, bias]).reshape(P, HEADS * SEQ)
    powers = np.zeros((2, TK), np.float32)
    for cols, unit in ((A_COLS, NB), (Q_COLS, NA * NB), (B_COLS, 1)):
        powers[1, cols] = np.arange(cols.stop - cols.start)
        powers[0, cols] = unit * powers[1, cols]
    times = np.ascontiguousarray(np.broadcast_to(powers.reshape(-1), (P, 2 * TK)))
    return {"ident": ident, "alibi": alibi, "times": times}


_INS = ["x", "L0_tok_A_abslog", "L0_tok_A_phase", "L0_attn_Wqkv", "L0_attn_Wo",
        "L0_ffn_A_w", "L0_ffn_B_w", "L0_ffn_Wq_w", "L0_ffn_keys"]


def kernel(**inputs):
    import concourse.bacc as bacc
    from concourse.bass_utils import run_bass_kernel_spmd

    nc = bacc.Bacc("TRN2", target_bir_lowering=False, num_devices=1)
    arrays, args = {}, []
    for name, a in [(n, inputs[n]) for n in _INS] + list(_constants().items()):
        a = np.ascontiguousarray(a)
        arrays[f"in_{name}"] = a
        args.append(nc.dram_tensor(f"in_{name}", a.shape, mybir.dt.from_np(a.dtype), kind="ExternalInput").ap())
    out = nc.dram_tensor("out_rows", [BATCH * SEQ, HID], F32, kind="ExternalOutput").ap()
    vit_layer(nc, *args, out)
    r = run_bass_kernel_spmd(nc, [arrays], core_ids=[0])
    return r.results[0]["out_rows"].reshape(BATCH, SEQ, HID)
```
